# Optimizing a Trainium2 kernel written in Bass

```python
import numpy as np
import jax
import jax.numpy as jnp

def _softmax(x, axis=-1):
    return jax.nn.softmax(x, axis=axis)

def _gelu(x):
    return jax.nn.gelu(x, approximate=True)

def _silu(x):
    return jax.nn.silu(x)

def _sigmoid(x):
    return jax.nn.sigmoid(x)

def _layernorm(x, axis=-1, eps=1e-05):
    m = jnp.mean(x, axis=axis, keepdims=True)
    v = jnp.var(x, axis=axis, keepdims=True)
    return (x - m) / jnp.sqrt(v + eps)

def _scatter_add(tgt, idx, src, axis=0):
    return tgt.at[idx].add(src)

def _segment_sum(src, seg, n):
    return jax.ops.segment_sum(src, seg, n)
kernel_name = 'mk_xattn_ffn_d1_seqx_r8_d582bb'

def setup_inputs(seed: int=0):
    np.random.seed(seed)
    _w = jnp.asarray

    def _rec_inputs():
        import jax
        import jax.numpy as jnp
        _rk = jax.random.key(seed)
        x = 7.22e-05 + 1 * jax.random.normal(jax.random.fold_in(_rk, 1), (64, 128, 128), jnp.float32)
        _lenS = 128 - jax.random.randint(jax.random.fold_in(_rk, 7), (64,), 0, max(1, 128 // 4) + 1, jnp.int32)
        _lenS2 = 120 - jax.random.randint(jax.random.fold_in(_rk, 8), (64,), 0, max(1, 120 // 4) + 1, jnp.int32)
        _ctx_1024P = jax.random.normal(jax.random.fold_in(_rk, 11), (64, 16, 128), jnp.float32)
        _ctx_1024c = jax.random.dirichlet(jax.random.fold_in(_rk, 511), 0.3 * jnp.ones((16,), jnp.float32), (64, 120))
        _ctx_1024t = jnp.einsum('bsk,bkd->bsd', _ctx_1024c, _ctx_1024P)
        _ctx_1024t = _ctx_1024t * jax.lax.rsqrt(jnp.mean(jnp.square(_ctx_1024t)) + 1e-12) * 0.953939
        ctx_1024 = 4.13588e-05 + 0.999923 * (_ctx_1024t + 0.3 * jax.random.normal(jax.random.fold_in(_rk, 611), (64, 120, 128), jnp.float32))
        return (x, ctx_1024)
    x, ctx_1024 = _rec_inputs()

    def _L0_xattn_setup():
        import jax, jax.numpy as jnp
        import numpy as np
        import math
        D_MODEL = 128
        D_K = 128
        D_V = 128
        B, S = (4, 256)
        key = jax.random.key(seed)
        ks = jax.random.split(key, 6)
        scale = 1.0 / math.sqrt(D_MODEL)
        return {'q': jax.random.normal(ks[0], (B, S, D_MODEL), dtype=jnp.float32), 'k': jax.random.normal(ks[1], (B, S, D_MODEL), dtype=jnp.float32), 'v': jax.random.normal(ks[2], (B, S, D_MODEL), dtype=jnp.float32), 'Wq': jax.random.normal(ks[3], (D_K, D_MODEL), dtype=jnp.float32) * scale, 'bq': jnp.zeros((D_K,), dtype=jnp.float32), 'Wk': jax.random.normal(ks[4], (D_K, D_MODEL), dtype=jnp.float32) * scale, 'bk': jnp.zeros((D_K,), dtype=jnp.float32), 'Wv': jax.random.normal(ks[5], (D_V, D_MODEL), dtype=jnp.float32) * scale, 'bv': jnp.zeros((D_V,), dtype=jnp.float32)}
    _L0_xattn_all = _L0_xattn_setup()
    _L0_xattn_in = {k: v for k, v in _L0_xattn_all.items() if k in ('Wq', 'bq', 'Wk', 'bk', 'Wv', 'bv')}
    del _L0_xattn_all

    def _L0_ffn_setup():
        import jax, jax.numpy as jnp
        import numpy as np
        B, S, H, E, I, MAX_K, A_HID = (2, 256, 128, 8, 336, 6, 50)
        key = jax.random.key(seed)
        ks = jax.random.split(key, 10)
        sc = 0.02
        return {'hidden_states': jax.random.normal(ks[0], (B, S, H), dtype=jnp.float32), 'router_w': jax.random.normal(ks[1], (E, H), dtype=jnp.float32) * sc, 'actor_w1': jax.random.normal(ks[2], (A_HID, H), dtype=jnp.float32) * sc, 'actor_b1': jnp.zeros((A_HID,), dtype=jnp.float32), 'actor_w2': jax.random.normal(ks[3], (MAX_K, A_HID), dtype=jnp.float32) * sc, 'actor_b2': jnp.zeros((MAX_K,), dtype=jnp.float32), 'gate_w': jax.random.normal(ks[4], (E, I, H), dtype=jnp.float32) * sc, 'up_w': jax.random.normal(ks[5], (E, I, H), dtype=jnp.float32) * sc, 'down_w': jax.random.normal(ks[6], (E, H, I), dtype=jnp.float32) * sc}
    _L0_ffn_all = _L0_ffn_setup()
    _L0_ffn_in = {k: v for k, v in _L0_ffn_all.items() if k in ('router_w', 'actor_w1', 'actor_b1', 'actor_w2', 'actor_b2', 'gate_w', 'up_w', 'down_w')}
    del _L0_ffn_all
    return {'x': x, 'ctx_1024': ctx_1024, 'L0_xattn_Wq': _L0_xattn_in['Wq'], 'L0_xattn_bq': _L0_xattn_in['bq'], 'L0_xattn_Wk': _L0_xattn_in['Wk'], 'L0_xattn_bk': _L0_xattn_in['bk'], 'L0_xattn_Wv': _L0_xattn_in['Wv'], 'L0_xattn_bv': _L0_xattn_in['bv'], 'L0_ffn_router_w': _L0_ffn_in['router_w'], 'L0_ffn_actor_w1': _L0_ffn_in['actor_w1'], 'L0_ffn_actor_b1': _L0_ffn_in['actor_b1'], 'L0_ffn_actor_w2': _L0_ffn_in['actor_w2'], 'L0_ffn_actor_b2': _L0_ffn_in['actor_b2'], 'L0_ffn_gate_w': _L0_ffn_in['gate_w'], 'L0_ffn_up_w': _L0_ffn_in['up_w'], 'L0_ffn_down_w': _L0_ffn_in['down_w']}

def reference(x, ctx_1024, L0_xattn_Wq, L0_xattn_bq, L0_xattn_Wk, L0_xattn_bk, L0_xattn_Wv, L0_xattn_bv, L0_ffn_router_w, L0_ffn_actor_w1, L0_ffn_actor_b1, L0_ffn_actor_w2, L0_ffn_actor_b2, L0_ffn_gate_w, L0_ffn_up_w, L0_ffn_down_w):
    import jax
    import jax.numpy as jnp

    def _L0_xattn_ref(q, k, v, Wq, bq, Wk, bk, Wv, bv):
        import jax, jax.numpy as jnp
        import numpy as np
        import math
        D_MODEL = 128
        D_K = 128
        D_V = 128
        B, S = (4, 256)
        qp = jnp.einsum('bsd,kd->bsk', q, Wq) + bq
        kp = jnp.einsum('bsd,kd->bsk', k, Wk) + bk
        vp = jnp.einsum('bsd,kd->bsk', v, Wv) + bv
        energies = jnp.einsum('bqk,bsk->bqs', qp, kp) / math.sqrt(D_K)
        weights = jax.nn.softmax(energies, axis=-1)
        out = jnp.einsum('bqs,bsv->bqv', weights, vp)
        return out

    def _L0_ffn_ref(hidden_states, router_w, actor_w1, actor_b1, actor_w2, actor_b2, gate_w, up_w, down_w):
        import jax, jax.numpy as jnp
        import numpy as np
        B, S, H, E, I, MAX_K, A_HID = (2, 256, 128, 8, 336, 6, 50)
        probs = jax.nn.softmax(jnp.einsum('bsh,eh->bse', hidden_states, router_w).astype(jnp.float32), axis=-1)
        a_h = jax.nn.gelu(jnp.einsum('bsh,ah->bsa', hidden_states, actor_w1) + actor_b1)
        actor_logits = jnp.clip(jnp.einsum('bsa,ka->bsk', a_h, actor_w2) + actor_b2, -30.0, 30.0)
        sampled_k = jnp.argmax(actor_logits, axis=-1) + 1
        order = jnp.argsort(-probs, axis=-1)
        rank = jnp.argsort(order, axis=-1)
        mask = rank < sampled_k[..., None]
        scores = jnp.where(mask, probs, 0.0).astype(hidden_states.dtype)
        out = jnp.zeros_like(hidden_states)
        for e in range(E):
            g = jnp.einsum('bsh,ih->bsi', hidden_states, gate_w[e])
            u = jnp.einsum('bsh,ih->bsi', hidden_states, up_w[e])
            y = jnp.einsum('bsi,hi->bsh', jax.nn.silu(g) * u, down_w[e])
            out = out + scores[..., e:e + 1] * y
        return out
    x = x + _L0_xattn_ref(_layernorm(x, axis=-1), ctx_1024, ctx_1024, L0_xattn_Wq, L0_xattn_bq, L0_xattn_Wk, L0_xattn_bk, L0_xattn_Wv, L0_xattn_bv)
    x = x + _L0_ffn_ref(_layernorm(x, axis=-1), L0_ffn_router_w, L0_ffn_actor_w1, L0_ffn_actor_b1, L0_ffn_actor_w2, L0_ffn_actor_b2, L0_ffn_gate_w, L0_ffn_up_w, L0_ffn_down_w)
    return x

_drawn_inputs = setup_inputs


def setup_inputs(seed=0):
    import zlib

    import numpy as np

    out = dict(_drawn_inputs(seed))
    spreads = {'L0_xattn_bq': (0.0, 0.365),
     'L0_xattn_bk': (0.0, 0.8),
     'L0_xattn_bv': (0.0, 0.1),
     'L0_ffn_actor_b1': (0.0, 0.8),
     'L0_ffn_actor_b2': (0.0, 0.8)}
    factors = {'L0_ffn_router_w': 8.0,
     'L0_ffn_actor_w1': 8.0,
     'L0_ffn_actor_w2': 8.0,
     'L0_ffn_gate_w': 8.0,
     'L0_ffn_up_w': 8.0,
     'L0_ffn_down_w': 8.0}
    for name, (base, spread) in spreads.items():
        noise = np.random.default_rng([zlib.crc32(name.encode()), seed]).standard_normal(out[name].shape)
        drawn = base * np.exp(spread * noise) if base else spread * noise
        out[name] = jnp.asarray(drawn.astype(out[name].dtype))
    for name, factor in factors.items():
        out[name] = (out[name] * factor).astype(out[name].dtype)
    return out
```

```python
from contextlib import ExitStack

import numpy as np

import concourse.bass as bass
from concourse import mybir

F32 = mybir.dt.float32
F16 = mybir.dt.float16
U32 = mybir.dt.uint32
ALU = mybir.AluOpType
ACT = mybir.ActivationFunctionType
AX = mybir.AxisListType

P = 128
BATCHES, CTX = 64, 120
BB = 4
NT = BB * P
NC = BB * CTX
BLOCKS = BATCHES // BB
EXPERTS, HIDDEN = 8, 336
ROWS = P // EXPERTS
TILES = HIDDEN // ROWS
ACTOR, KMAX = 50, 6
EPS = 1e-5
GELU_C, GELU_A = 0.7978845608028654, 0.044715
SCALE = float(P) ** -0.5

G_BANKS, U_BANKS = 2, 3
RING, HRING = 3, 6
DOWN_LAG = 4
PAIR = 2 * TILES

W_TOP = 256.0
H_SCALE = 2.0 ** -7
S_SCALE = 256.0

ROUTE_STEPS = 16


def program(nc, x, ctx_t, wcols, pcols, bv, b2, w2t, gate_t, up_t, down_t, ident, ident16, sel, tri, iota, out):
    x_blocks = x.rearrange("(t b p) d -> t p b d", b=BB, p=P)
    out_blocks = out.rearrange("(t b p) d -> t p b d", b=BB, p=P)
    ctx_blocks = ctx_t.rearrange("p (t n) -> t p n", n=NC)

    with ExitStack() as stack:
        def sb(name, shape, dt=F32):
            return stack.enter_context(nc.sbuf_tensor(name, shape, dt))

        def sem(name):
            return stack.enter_context(nc.semaphore(name))

        bank = [stack.enter_context(nc.psum_tensor(f"bank{k}", [P, 512], F32)) for k in range(8)]

        wcol_sb = sb("wcol_sb", [P, 3 * P + EXPERTS + ACTOR])
        wq_t, wk_t, wv_t = (wcol_sb[:, k * P:(k + 1) * P] for k in range(3))
        router_t = wcol_sb[:, 3 * P:3 * P + EXPERTS]
        w1_t = wcol_sb[:, 3 * P + EXPERTS:]
        pcol_sb = sb("pcol_sb", [P, 3])
        bq_scaled = sb("bq_scaled", [P, 1])
        bv_sb = sb("bv_sb", [P, P])
        b2_sb = sb("b2_sb", [P, KMAX])
        w2_sb = sb("w2_sb", [ACTOR, KMAX])
        ident_sb = sb("ident_sb", [P, P])
        ident16_sb = sb("ident16_sb", [P, P], F16)
        sel_sb = sb("sel_sb", [2 * EXPERTS, P], F16)
        tri_sb = sb("tri_sb", [P, EXPERTS, EXPERTS])
        iota_sb = sb("iota_sb", [P, KMAX])
        eps_sb = sb("eps_sb", [P, BB])
        neg_half = sb("neg_half", [P, BB])
        work = sb("work", [P, 2 * TILES * P])
        raw = [work[:, 0:TILES * P], work[:, TILES * P:], sb("raw_down", [P, TILES * P])[:]]
        w_hi = [sb(f"{n}_hi", [P, TILES * P], F16) for n in ("gate", "up", "down")]
        w_lo = [sb(f"{n}_lo", [P, TILES * P], F16) for n in ("gate", "up", "down")]
        w_abs = sb("w_abs", [P, 3])
        w_top = sb("w_top", [P, 3])
        w_pow = sb("w_pow", [P, 3])
        w_inv = sb("w_inv", [P, 3])
        w_mul = sb("w_mul", [P, 3])
        silu_scale = sb("silu_scale", [P, 1])
        h_scale = sb("h_scale", [P, 1])
        y_scale = sb("y_scale", [P, 2])

        x2_all = sb("x2_all", [P, BLOCKS, BB, P])
        xn_hi = sb("xn_hi", [P, BLOCKS, NT], F16)
        xn_lo = sb("xn_lo", [P, BLOCKS, NT], F16)
        route_exp = sb("route_exp", [P, BLOCKS, BB, EXPERTS])
        actor_log = sb("actor_log", [P, BLOCKS, BB, KMAX])

        x_in = [sb(f"x_in{k}", [P, BB, P]) for k in range(2)]
        ctx_in = [sb(f"ctx_in{k}", [P, NC]) for k in range(2)]
        stats1 = sb("stats1", [P, BB, 6])
        mv1 = [sb(f"mv1_{k}", [P, BB, 2]) for k in range(2)]
        ve1 = sb("ve1", [P, BB])
        rstd1 = sb("rstd1", [P, BB])
        xn_nat = [sb(f"xn_nat{k}", [P, BB, P]) for k in range(2)]
        xb = [sb(f"xb{k}", [P, BB, P]) for k in range(2)]
        xn_t = sb("xn_t", [P, NT])
        q_t = sb("q_t", [P, NT])
        k_t = sb("k_t", [P, NC])
        v_sb = [sb(f"v_sb{k}", [CTX, BB * P]) for k in range(2)]
        neg_max = [sb(f"neg_max{k}", [P, BB]) for k in range(2)]
        probs = sb("probs", [P, BB, CTX])
        sums = [sb(f"sums{k}", [P, BB]) for k in range(2)]
        inv_sum = sb("inv_sum", [P, BB])
        probs_t = sb("probs_t", [CTX, BB * P])
        stats2 = sb("stats2", [P, BB, 6])
        mv2 = [sb(f"mv2_{k}", [P, BB, 2]) for k in range(2)]
        ve2 = sb("ve2", [P, BB])
        rstd2 = [sb(f"rstd2_{k}", [P, BB]) for k in range(2)]
        xn2_nat = sb("xn2_nat", [P, BB, P])
        xn2_t = sb("xn2_t", [P, NT])
        route_max = sb("route_max", [P, BB])
        a_sb = sb("a_sb", [ACTOR, NT])
        shared = [sb(f"shared{k}", [P, NT]) for k in range(5)]
        a_sq, a_poly, a_arg, a_tanh, a_gelu2 = (buf[0:ACTOR, :] for buf in shared)
        al_raw = sb("al_raw", [P, BB, KMAX])

        silu, weighted, hid = ([work[:, (r * RING + k) * NT:(r * RING + k + 1) * NT] for k in range(RING)]
                               for r in range(3))
        hid_hi = [sb(f"hid_hi{k}", [P, NT], F16) for k in range(HRING)]
        hid_lo = [sb(f"hid_lo{k}", [P, NT], F16) for k in range(HRING)]
        p_sum = sb("p_sum", [P, BB])
        p_inv = sb("p_inv", [P, BB])
        prob = sb("prob", [P, BB, EXPERTS])
        al_max = sb("al_max", [P, BB])
        al_less = sb("al_less", [P, BB, KMAX])
        al_cand = sb("al_cand", [P, BB, KMAX])
        k_less1 = sb("k_less1", [P, BB])
        beats = sb("beats", [P, BB, EXPERTS, EXPERTS])
        ties = sb("ties", [P, BB, EXPERTS, EXPERTS])
        ties_lo = sb("ties_lo", [P, BB, EXPERTS, EXPERTS])
        ahead = sb("ahead", [P, BB, EXPERTS, EXPERTS])
        rank = sb("rank", [P, BB, EXPERTS])
        chosen = sb("chosen", [P, BB, EXPERTS])
        score = sb("score", [P, BB, EXPERTS])
        score16 = sb("score16", [P, BB, 2 * EXPERTS], F16)
        score_t = sb("score_t", [2 * EXPERTS, NT], F16)
        score_bc = [shared[k][:] for k in range(2)]
        y_sb = shared[2][:]
        out_sb = [shared[3 + k][:].rearrange("p (b d) -> p b d", b=BB) for k in range(2)]

        consts_in = sem("consts_in")
        weights_in = [sem(f"weights_in{k}") for k in range(3)]
        x_loaded = [sem(f"x_loaded{k}") for k in range(2)]
        ctx_loaded = [sem(f"ctx_loaded{k}") for k in range(2)]
        setup_vec = sem("setup_vec")
        setup_pool = sem("setup_pool")
        w_stat = sem("w_stat")
        w_all = sem("w_all")
        w_chain = sem("w_chain")
        w_hi_done = sem("w_hi_done")
        w_split = sem("w_split")
        ln1_stats, ln1_mv, ln1_ve, ln1_rstd, xn_ready, xb_ready = (
            sem(n) for n in ("ln1_stats", "ln1_mv", "ln1_ve", "ln1_rstd", "xn_ready", "xb_ready"))
        t1_done, xnt_ready, kp_done, kt_ready, vp_done, v_ready, qp_done, qt_ready = (
            sem(n) for n in ("t1_done", "xnt_ready", "kp_done", "kt_ready", "vp_done", "v_ready", "qp_done",
                             "qt_ready"))
        e_done, max_ready, exp_done, pt_done, ptt_ready, o_done, inv_ready, x2_ready = (
            sem(n) for n in ("e_done", "max_ready", "exp_done", "pt_done", "ptt_ready", "o_done", "inv_ready",
                             "x2_ready"))
        ln2_stats, ln2_mv, ln2_ve, ln2_rstd, xn2_ready, t2_done, xn2t_ready, hi_ready, lo_ready = (
            sem(n) for n in ("ln2_stats", "ln2_mv", "ln2_ve", "ln2_rstd", "xn2_ready", "t2_done", "xn2t_ready",
                             "hi_ready", "lo_ready"))
        ah_done, a_ready, sq_ready, poly_ready, arg_ready, tanh_ready, gelu_ready, al_done, al_add, al_ready = (
            sem(n) for n in ("ah_done", "a_ready", "sq_ready", "poly_ready", "arg_ready", "tanh_ready",
                             "gelu_ready", "al_done", "al_add", "al_ready"))
        r_done, rmax_ready, rsub_ready, rexp_ready = (
            sem(n) for n in ("r_done", "rmax_ready", "rsub_ready", "rexp_ready"))
        gate_done, up_done, silu_ready, weighted_ready, hid_ready, hid_hi_ready, hid_lo_ready, down_done = (
            sem(n) for n in ("gate_done", "up_done", "silu_ready", "weighted_ready", "hid_ready", "hid_hi_ready",
                             "hid_lo_ready", "down_done"))
        route_step, st_done, st_ready, bc_done, bc_ready, y_ready, yt_done, out_ready = (
            sem(n) for n in ("route_step", "st_done", "st_ready", "bc_done", "bc_ready", "y_ready", "yt_done",
                             "out_ready"))
        stored = [sem(f"stored{k}") for k in range(2)]

        N_CONSTS = 11

        def wait(eng, s, value):
            if not isinstance(value, int) or value > 0:
                eng.wait_ge(s, value)

        def live(slot, lag):
            return not isinstance(slot, int) or 0 <= slot - lag < BLOCKS

        def slots(eng, body):
            for s in range(-1, 4):
                body(s, s % 2)
            with eng.Fori(2, BLOCKS // 2 - 1) as i:
                body(2 * i, 0)
                body(2 * i + 1, 1)
            for s in range(BLOCKS - 2, BLOCKS + 3):
                body(s, s % 2)

        block = stack.enter_context(nc.Block())

        @block.sync
        def _(sp):
            for dst, src in ((wcol_sb[:], wcols), (pcol_sb[:], pcols), (ident_sb[:], ident),
                             (bv_sb[:], bv.partition_broadcast(P)), (b2_sb[:], b2.partition_broadcast(P)),
                             (w2_sb[:], w2t), (ident16_sb[:], ident16), (sel_sb[:], sel),
                             (tri_sb[:], tri), (iota_sb[:], iota)):
                sp.dma_start(dst, src).then_inc(consts_in, 16)

            def loads(b, par, n):
                wait(sp, xb_ready, b - 1)
                sp.dma_start(x_in[par][:], x_blocks[b]).then_inc(x_loaded[par], 16)
                wait(sp, vp_done, b - 1)
                sp.dma_start(ctx_in[par][:], ctx_blocks[b]).then_inc(ctx_loaded[par], 16)

            loads(0, 0, 0)
            loads(1, 1, 0)
            for k, w in enumerate((gate_t, up_t, down_t)):
                sp.dma_start(raw[k], w).then_inc(weights_in[k], 16)
            with sp.Fori(1, BLOCKS // 2) as i:
                loads(2 * i, 0, i)
                loads(2 * i + 1, 1, i)

            with sp.Fori(0, BLOCKS // 2) as i:
                for par in range(2):
                    sp.wait_ge(out_ready, 2 * i + par + 1)
                    sp.dma_start(out_blocks[2 * i + par], out_sb[par]).then_inc(stored[par], 16)
            for par in range(2):
                sp.wait_ge(stored[par], 16 * (BLOCKS // 2))

        @block.tensor
        def _(pe):
            mm = nc.tensor.matmul

            def slot(s, par):
                if live(s, 0):
                    pe.wait_ge(xn_ready, s + 1)
                    wait(pe, xn2t_ready, s - 3 + 1)
                    for b in range(BB):
                        last = nc.tensor.transpose(bank[0][:, b * P:(b + 1) * P], xn_nat[par][:, b, :], ident_sb[:])
                    last.then_inc(t1_done, 1)
                if live(s, 1):
                    pe.wait_ge(qt_ready, s)
                    wait(pe, exp_done, BB * (s - 1))
                    for b in range(BB):
                        last = mm(bank[4][:, b * CTX:(b + 1) * CTX], q_t[:, b * P:(b + 1) * P],
                                  k_t[:, b * CTX:(b + 1) * CTX], start=True, stop=True)
                    last.then_inc(e_done, 1)
                if live(s, 0):
                    pe.wait_ge(ctx_loaded[par], 8 * (s - par) + 16)
                    wait(pe, kt_ready, s)
                    wait(pe, rsub_ready, s - 3 + 1)
                    mm(bank[1][:, 0:NC], wk_t, ctx_in[par][:], start=True, stop=True).then_inc(kp_done, 1)
                    wait(pe, v_ready, s)
                    for b in range(BB):
                        last = mm(bank[2][0:CTX, b * P:(b + 1) * P], ctx_in[par][:, b * CTX:(b + 1) * CTX], wv_t,
                                  start=True, stop=True)
                    last.then_inc(vp_done, 1)
                    pe.wait_ge(xnt_ready, s + 1)
                    wait(pe, qt_ready, s)
                    mm(bank[3][:], wq_t, xn_t[:], start=True, stop=True).then_inc(qp_done, 1)
                if live(s, 1):
                    pe.wait_ge(exp_done, BB * s)
                    wait(pe, ptt_ready, s - 1)
                    for b in range(BB):
                        last = nc.tensor.transpose(bank[5][0:CTX, b * P:(b + 1) * P], probs[:, b, :], ident_sb[:])
                    last.then_inc(pt_done, 1)
                if live(s, 2):
                    pe.wait_ge(xn2_ready, s - 1)
                    wait(pe, xnt_ready, s + 1 if not isinstance(s, int) else min(s + 1, BLOCKS))
                    for b in range(BB):
                        last = nc.tensor.transpose(bank[0][:, b * P:(b + 1) * P], xn2_nat[:, b, :], ident_sb[:])
                    last.then_inc(t2_done, 1)
                if live(s, 1):
                    pe.wait_ge(ptt_ready, s)
                    pe.wait_ge(v_ready, s)
                    wait(pe, x2_ready, s - 1)
                    for b in range(BB):
                        last = mm(bank[6][:, b * P:(b + 1) * P], probs_t[:, b * P:(b + 1) * P],
                                  v_sb[1 - par][:, b * P:(b + 1) * P], start=True, stop=True)
                    last.then_inc(o_done, 1)
                if live(s, 3):
                    pe.wait_ge(gelu_ready, s - 3 + 1)
                    for b in range(BB):
                        last = mm(bank[7][:, b * KMAX:(b + 1) * KMAX], a_gelu2[:, b * P:(b + 1) * P], w2_sb[:],
                                  start=True, stop=True)
                    last.then_inc(al_done, 1)
                if live(s, 2):
                    pe.wait_ge(xn2t_ready, s - 1)
                    wait(pe, al_add, s - 2)
                    mm(bank[7][0:ACTOR, :], w1_t, xn2_t[:], start=True, stop=True).then_inc(ah_done, 1)
                    wait(pe, kt_ready, s + 1 if not isinstance(s, int) else min(s + 1, BLOCKS))
                    for b in range(BB):
                        last = mm(bank[1][:, NC + b * EXPERTS:NC + (b + 1) * EXPERTS], xn2_t[:, b * P:(b + 1) * P],
                                  router_t, start=True, stop=True)
                    last.then_inc(r_done, 1)

            pe.wait_ge(consts_in, 16 * (N_CONSTS - 1))
            slots(pe, slot)

            def score_transposes(t):
                pe.wait_ge(route_step, ROUTE_STEPS * (t + 1))
                wait(pe, out_ready, t - 2)
                for b in range(BB):
                    last = nc.tensor.transpose(bank[7][0:2 * EXPERTS, :].bitcast(F16)[:, b * P:(b + 1) * P],
                                               score16[:, b, :], ident16_sb[:])
                last.then_inc(st_done, 1)

            def score_broadcast(t):
                pe.wait_ge(st_ready, t + 1)
                mm(bank[7][:], sel_sb[:], score_t[:], start=True, stop=True).then_inc(bc_done, 1)

            def result_transposes(t):
                pe.wait_ge(y_ready, t + 1)
                wait(pe, bc_ready, t + 3 if not isinstance(t, int) else min(t + 3, BLOCKS))
                for b in range(BB):
                    last = nc.tensor.transpose(bank[7][:, b * P:(b + 1) * P], y_sb[:, b * P:(b + 1) * P], ident_sb[:])
                last.then_inc(yt_done, 1)

            def split_product(dst, w, tile, hi, lo, start, stop):
                cols = slice(tile * P, (tile + 1) * P)
                mm(dst, w_hi[w][:, cols], lo, start=start, stop=False)
                mm(dst, w_lo[w][:, cols], hi, start=False, stop=False)
                return mm(dst, w_hi[w][:, cols], hi, start=False, stop=stop)

            def down(i, p):
                j, par = p % TILES, (p // TILES) % 2
                tile = PAIR * i + p
                pe.wait_ge(hid_lo_ready, tile + 1)
                if j == 0:
                    wait(pe, y_ready, 2 * i + par - 1)
                split_product(bank[5 + par][:], 2, j, hid_hi[p % HRING][:], hid_lo[p % HRING][:],
                              j == 0, j == TILES - 1).then_inc(down_done, 1)

            def pair(i, first):
                for p in range(PAIR):
                    par, j = divmod(p, TILES)
                    t = 2 * i + par
                    tile = PAIR * i + p
                    wait(pe, silu_ready, tile - G_BANKS + 1)
                    split_product(bank[p % G_BANKS][:], 0, j, xn_hi[:, t, :], xn_lo[:, t, :], True, True)\
                        .then_inc(gate_done, 1)
                    wait(pe, hid_ready, tile - U_BANKS + 1)
                    split_product(bank[2 + p % U_BANKS][:], 1, j, xn_hi[:, t, :], xn_lo[:, t, :], True, True)\
                        .then_inc(up_done, 1)
                    if p >= DOWN_LAG or not first:
                        down(i, p - DOWN_LAG)
                    if j == 12 and not (par == 1 and isinstance(i, int) and i == BLOCKS // 2 - 1):
                        score_transposes(t + 1)
                    if j == 14 and not (par == 1 and isinstance(i, int) and i == BLOCKS // 2 - 1):
                        score_broadcast(t + 1)
                    if j == 18 and not (first and par == 0):
                        result_transposes(t - 1)

            pe.wait_ge(w_split, 3)
            pe.wait_ge(lo_ready, BLOCKS)
            pe.wait_ge(hi_ready, BLOCKS)
            pe.wait_ge(al_ready, BLOCKS)
            pe.wait_ge(rsub_ready, BLOCKS)
            pe.wait_ge(x2_ready, BLOCKS)
            score_transposes(0)
            score_broadcast(0)
            pe.wait_ge(bc_ready, 1)
            pair(0, True)
            with pe.Fori(1, BLOCKS // 2 - 1) as i:
                pair(i, False)
            pair(BLOCKS // 2 - 1, False)
            for p in range(PAIR - DOWN_LAG, PAIR):
                down(BLOCKS // 2 - 1, p)
            result_transposes(BLOCKS - 1)

        @block.scalar
        def _(act):
            af = nc.scalar.activation

            def slot(s, par):
                if live(s, 1):
                    pe_prev = 1 - par
                    act.wait_ge(max_ready, s)
                    wait(act, pt_done, s - 1)
                    wait(act, inv_ready, s - 2)
                    for b in range(BB):
                        af(probs[:, b, :], bank[4][:, b * CTX:(b + 1) * CTX], ACT.Exp, bias=neg_max[pe_prev][:, b:b + 1],
                           accum_out=sums[pe_prev][:, b:b + 1]).then_inc(exp_done, 1)
                if live(s, 0):
                    act.wait_ge(t1_done, s + 1)
                    wait(act, qp_done, s)
                    af(xn_t[:], bank[0][:], ACT.Copy).then_inc(xnt_ready, 1)
                    act.wait_ge(kp_done, s + 1)
                    wait(act, e_done, s)
                    af(k_t[:], bank[1][:, 0:NC], ACT.Identity, bias=pcol_sb[:, 1:2]).then_inc(kt_ready, 1)
                    act.wait_ge(qp_done, s + 1)
                    af(q_t[:], bank[3][:], ACT.Identity, bias=bq_scaled[:], scale=SCALE).then_inc(qt_ready, 1)
                if live(s, 3):
                    act.wait_ge(arg_ready, s - 2)
                    wait(act, gelu_ready, s - 3)
                    af(a_tanh, a_arg, ACT.Tanh, scale=GELU_C).then_inc(tanh_ready, 1)
                if live(s, 1):
                    act.wait_ge(pt_done, s)
                    wait(act, o_done, s - 1)
                    af(probs_t[:], bank[5][0:CTX, :], ACT.Copy).then_inc(ptt_ready, 1)
                if live(s, 2):
                    act.wait_ge(t2_done, s - 1)
                    wait(act, r_done, s - 2)
                    wait(act, hi_ready, s - 2)
                    wait(act, lo_ready, s - 2)
                    af(xn2_t[:], bank[0][:], ACT.Copy).then_inc(xn2t_ready, 1)
                    act.wait_ge(ah_done, s - 1)
                    wait(act, gelu_ready, s - 2)
                    af(a_sb[:], bank[7][0:ACTOR, :], ACT.Identity, bias=pcol_sb[0:ACTOR, 2:3]).then_inc(a_ready, 1)
                    act.wait_ge(a_ready, s - 1)
                    wait(act, poly_ready, s - 2)
                    af(a_sq, a_sb[:], ACT.Square, scale=GELU_A ** 0.5).then_inc(sq_ready, 1)

            act.wait_ge(consts_in, 16 * (N_CONSTS - 1))
            act.wait_ge(setup_vec, 2)
            nc.scalar.preload_act_table(ACT.Exp)
            slots(act, slot)
            act.wait_ge(rsub_ready, BLOCKS)
            af(route_exp[:], route_exp[:], ACT.Exp).then_inc(rexp_ready, 1)
            act.wait_ge(w_chain, 4)

            def score_copy(t):
                act.wait_ge(st_done, t + 1)
                wait(act, bc_done, t)
                af(score_t[:], bank[7][0:2 * EXPERTS, :].bitcast(F16)[:, 0:NT], ACT.Copy).then_inc(st_ready, 1)

            def score_spread(t, par):
                act.wait_ge(bc_done, t + 1)
                wait(act, weighted_ready, TILES * (t - 1))
                af(score_bc[par], bank[7][:], ACT.Copy, scale=1.0 / S_SCALE).then_inc(bc_ready, 1)

            def result_copy(t, par):
                act.wait_ge(down_done, TILES * (t + 1))
                wait(act, yt_done, t)
                af(y_sb, bank[5 + par][:], ACT.Copy, scale=y_scale[:, 1:2]).then_inc(y_ready, 1)

            def high_part(i, p):
                tile = PAIR * i + p
                act.wait_ge(hid_ready, tile + 1)
                wait(act, down_done, tile - HRING + 1)
                af(hid_hi[p % HRING][:], hid[p % RING], ACT.Copy).then_inc(hid_hi_ready, 1)

            def pair(i, first):
                for p in range(PAIR):
                    par, j = divmod(p, TILES)
                    t = 2 * i + par
                    tile = PAIR * i + p
                    act.wait_ge(gate_done, tile + 1)
                    wait(act, weighted_ready, tile - RING + 1)
                    af(silu[p % RING], bank[p % G_BANKS][:], ACT.Silu, scale=silu_scale[:]).then_inc(silu_ready, 1)
                    if p >= 2 or not first:
                        high_part(i, p - 2)
                    if j == 12 and not (par == 1 and isinstance(i, int) and i == BLOCKS // 2 - 1):
                        score_copy(t + 1)
                    if j == 14 and not (par == 1 and isinstance(i, int) and i == BLOCKS // 2 - 1):
                        score_spread(t + 1, 1 - par)
                    if j == DOWN_LAG + 1 and not (first and par == 0):
                        result_copy(t - 1, 1 - par)

            nc.scalar.preload_act_table(ACT.Silu)
            score_copy(0)
            score_spread(0, 0)
            pair(0, True)
            with act.Fori(1, BLOCKS // 2 - 1) as i:
                pair(i, False)
            pair(BLOCKS // 2 - 1, False)
            for p in range(PAIR - 2, PAIR):
                high_part(BLOCKS // 2 - 1, p)
            result_copy(BLOCKS - 1, 1)

        @block.gpsimd
        def _(pool):
            g = nc.gpsimd
            g.memset(eps_sb[:], EPS).then_inc(setup_pool, 1)
            g.memset(neg_half[:], -0.5).then_inc(setup_pool, 1)
            pool.wait_ge(setup_pool, 2)
            pool.wait_ge(consts_in, 16 * (N_CONSTS - 1))

            def slot(s, par):
                nxt = 1 - par
                if live(s, -1):
                    pool.wait_ge(ln1_mv, s + 2)
                    wait(pool, xn_ready, s + 1)
                    g.tensor_tensor(ve1[:], mv1[nxt][:, :, 1], eps_sb[:], ALU.add).then_inc(ln1_ve, 1)
                    pool.wait_ge(ln1_ve, s + 2)
                    g.tensor_tensor(rstd1[:], ve1[:], neg_half[:], ALU.pow).then_inc(ln1_rstd, 1)
                    pool.wait_ge(ln1_rstd, s + 2)
                    wait(pool, t1_done, s)
                if live(s, 3):
                    pool.wait_ge(sq_ready, s - 2)
                    wait(pool, arg_ready, s - 3)
                    g.tensor_tensor(a_poly, a_sq, a_sb[:], ALU.mult).then_inc(poly_ready, 1)
                if live(s, -1):
                    for b in range(BB):
                        last = g.tensor_scalar(xn_nat[nxt][:, b, :], x_in[nxt][:, b, :], mv1[nxt][:, b, 0:1],
                                               rstd1[:, b:b + 1], ALU.subtract, ALU.mult)
                    last.then_inc(xn_ready, 1)
                if live(s, 3):
                    pool.wait_ge(poly_ready, s - 2)
                    wait(pool, tanh_ready, s - 3)
                    g.tensor_tensor(a_arg, a_poly, a_sb[:], ALU.add).then_inc(arg_ready, 1)
                if live(s, -1):
                    wait(pool, x2_ready, s)
                    g.tensor_tensor(xb[nxt][:], x_in[nxt][:], bv_sb[:].unsqueeze(1).broadcast_to([P, BB, P]), ALU.add)\
                        .then_inc(xb_ready, 1)
                if live(s, 1):
                    pool.wait_ge(ln2_mv, s)
                    wait(pool, ln2_rstd, s - 1)
                    g.tensor_tensor(ve2[:], mv2[1 - par][:, :, 1], eps_sb[:], ALU.add).then_inc(ln2_ve, 1)
                    pool.wait_ge(ln2_ve, s)
                    wait(pool, xn2_ready, s - 2)
                    g.tensor_tensor(rstd2[1 - par][:], ve2[:], neg_half[:], ALU.pow).then_inc(ln2_rstd, 1)
                if live(s, 2):
                    pool.wait_ge(hi_ready, s - 1)
                    g.tensor_tensor(xn_lo[:, s - 2, :], xn2_t[:], xn_hi[:, s - 2, :], ALU.subtract).then_inc(lo_ready, 1)

            slots(pool, slot)
            pool.wait_ge(w_stat, 3)
            g.partition_all_reduce(w_top[:], w_abs[:], P, bass.bass_isa.ReduceOp.max).then_inc(w_all, 1)

            with pool.Fori(0, BLOCKS // 2) as i:
                for p in range(PAIR):
                    par, j = divmod(p, TILES)
                    tile = PAIR * i + p
                    if j == 0:
                        pool.wait_ge(bc_ready, 2 * i + par + 1)
                    pool.wait_ge(silu_ready, tile + 1)
                    pool.wait_ge(up_done, tile + 1)
                    g.tensor_tensor(weighted[p % RING], silu[p % RING], score_bc[par], ALU.mult)\
                        .then_inc(weighted_ready, 1)

        @block.vector
        def _(dve):
            v = nc.vector

            def slot(s, par):
                if live(s, 2):
                    dve.wait_ge(ln2_rstd, s - 1)
                    wait(dve, t2_done, s - 2)
                    for b in range(BB):
                        last = v.tensor_scalar(xn2_nat[:, b, :], x2_all[:, s - 2, b, :], mv2[par][:, b, 0:1],
                                               rstd2[par][:, b:b + 1], ALU.subtract, ALU.mult)
                    last.then_inc(xn2_ready, 1)
                if live(s, 1):
                    dve.wait_ge(e_done, s)
                    wait(dve, exp_done, BB * (s - 2))
                    v.tensor_reduce(neg_max[1 - par][:], bank[4][:, 0:NC].rearrange("p (b n) -> p b n", b=BB), AX.X,
                                    ALU.max, negate=True).then_inc(max_ready, 1)
                nxt = 1 - par
                if live(s, -1):
                    wait(dve, ln1_mv, s + 1)
                    dve.wait_ge(x_loaded[nxt], 8 * (s + 1 - nxt) + 16)
                    for b in range(BB):
                        last = v.bn_stats(stats1[:, b, :], x_in[nxt][:, b, :])
                    last.then_inc(ln1_stats, 1)
                    dve.wait_ge(ln1_stats, s + 2)
                    wait(dve, xn_ready, s)
                if live(s, 0):
                    dve.wait_ge(vp_done, s + 1)
                    wait(dve, o_done, s - 1)
                    v.tensor_copy(v_sb[par][:], bank[2][0:CTX, :]).then_inc(v_ready, 1)
                if live(s, -1):
                    for b in range(BB):
                        last = v.bn_aggr(mv1[nxt][:, b, :], stats1[:, b, :])
                    last.then_inc(ln1_mv, 1)
                if live(s, 3):
                    dve.wait_ge(tanh_ready, s - 2)
                    wait(dve, al_done, s - 3)
                    v.scalar_tensor_tensor(a_gelu2, a_tanh, 1.0, a_sb[:], ALU.add, ALU.mult)\
                        .then_inc(gelu_ready, 1)
                if live(s, 2):
                    dve.wait_ge(xn2t_ready, s - 1)
                    v.tensor_copy(xn_hi[:, s - 2, :], xn2_t[:]).then_inc(hi_ready, 1)
                if live(s, 3):
                    dve.wait_ge(al_done, s - 2)
                    wait(dve, al_ready, s - 3)
                    v.scalar_tensor_tensor(al_raw[:], bank[7][:, 0:BB * KMAX].rearrange("p (b k) -> p b k", b=BB), 0.5,
                                           b2_sb[:].unsqueeze(1).broadcast_to([P, BB, KMAX]), ALU.mult, ALU.add)\
                        .then_inc(al_add, 1)
                    dve.wait_ge(al_add, s - 2)
                    v.tensor_scalar(actor_log[:, s - 3, :, :], al_raw[:], -30.0, 30.0, ALU.max, ALU.min)\
                        .then_inc(al_ready, 1)
                if live(s, 1):
                    dve.wait_ge(exp_done, BB * s)
                    wait(dve, x2_ready, s - 1)
                    v.reciprocal(inv_sum[:], sums[1 - par][:]).then_inc(inv_ready, 1)
                    dve.wait_ge(o_done, s)
                    dve.wait_ge(xb_ready, s)
                    dve.wait_ge(inv_ready, s)
                    for b in range(BB):
                        last = v.scalar_tensor_tensor(x2_all[:, s - 1, b, :], bank[6][:, b * P:(b + 1) * P],
                                                      inv_sum[:, b:b + 1], xb[1 - par][:, b, :], ALU.mult, ALU.add)
                    last.then_inc(x2_ready, 1)
                    dve.wait_ge(x2_ready, s)
                    wait(dve, ln2_mv, s - 1)
                if live(s, 2):
                    logits = bank[1][:, NC:NC + BB * EXPERTS].rearrange("p (b e) -> p b e", b=BB)
                    dve.wait_ge(r_done, s - 1)
                    wait(dve, rsub_ready, s - 2)
                    v.tensor_reduce(route_max[:], logits, AX.X, ALU.max).then_inc(rmax_ready, 1)
                if live(s, 1):
                    for b in range(BB):
                        last = v.bn_stats(stats2[:, b, :], x2_all[:, s - 1, b, :])
                    last.then_inc(ln2_stats, 1)
                    dve.wait_ge(ln2_stats, s)
                if live(s, 2):
                    dve.wait_ge(rmax_ready, s - 1)
                    v.tensor_tensor(route_exp[:, s - 2, :, :], logits,
                                    route_max[:].unsqueeze(2).broadcast_to([P, BB, EXPERTS]), ALU.subtract)\
                        .then_inc(rsub_ready, 1)
                if live(s, 1):
                    for b in range(BB):
                        last = v.bn_aggr(mv2[1 - par][:, b, :], stats2[:, b, :])
                    last.then_inc(ln2_mv, 1)

            dve.wait_ge(consts_in, 16 * (N_CONSTS - 1))
            v.tensor_scalar(bq_scaled[:], pcol_sb[:, 0:1], SCALE, None, ALU.mult).then_inc(setup_vec, 2)
            slots(dve, slot)

            for k in range(3):
                dve.wait_ge(weights_in[k], 16)
                v.tensor_reduce(w_abs[:, k:k + 1], raw[k], AX.X, ALU.max, apply_absolute_value=True)\
                    .then_inc(w_stat, 1)
            dve.wait_ge(w_all, 1)
            v.tensor_scalar(w_pow[:], w_top[:], 1e-30, None, ALU.max).then_inc(w_chain, 1)
            dve.wait_ge(w_chain, 1)
            v.tensor_scalar(w_pow[:].bitcast(U32), w_pow[:].bitcast(U32), 0x7F800000, None, ALU.bitwise_and)\
                .then_inc(w_chain, 1)
            dve.wait_ge(w_chain, 2)
            v.reciprocal(w_inv[:], w_pow[:]).then_inc(w_chain, 1)
            dve.wait_ge(w_chain, 3)
            v.tensor_scalar(w_mul[:], w_inv[:], W_TOP / 2, None, ALU.mult).then_inc(w_split, 1)
            v.tensor_scalar(silu_scale[:], w_pow[:, 0:1], 2 / W_TOP, None, ALU.mult)
            v.tensor_scalar(h_scale[:], w_inv[:, 0:1], H_SCALE / 2, None, ALU.mult)
            v.tensor_scalar(y_scale[:, 0:1], w_pow[:, 0:1], w_pow[:, 1:2], 8.0 / (W_TOP * W_TOP * H_SCALE),
                            ALU.mult, ALU.mult).then_inc(w_split, 1)
            dve.wait_ge(w_split, 2)
            v.tensor_scalar(y_scale[:, 1:2], y_scale[:, 0:1], w_pow[:, 2:3], None, ALU.mult).then_inc(w_chain, 1)
            for k in range(3):
                v.tensor_scalar(w_hi[k][:], raw[k], w_mul[:, k:k + 1], None, ALU.mult).then_inc(w_hi_done, 1)
                dve.wait_ge(w_hi_done, k + 1)
                last = v.scalar_tensor_tensor(w_lo[k][:], raw[k], w_mul[:, k:k + 1], w_hi[k][:], ALU.mult,
                                              ALU.subtract)
            last.then_inc(w_split, 1)

            def step(ins, t, n):
                ins.then_inc(route_step, 1)
                dve.wait_ge(route_step, ROUTE_STEPS * t + n)

            def over(col, n):
                return col.unsqueeze(2).broadcast_to([P, BB, n])

            def route_probs(t):
                step(v.tensor_reduce(p_sum[:], route_exp[:, t, :, :], AX.X, ALU.add), t, 1)
                step(v.reciprocal(p_inv[:], p_sum[:]), t, 2)
                step(v.tensor_tensor(prob[:], route_exp[:, t, :, :], over(p_inv[:], EXPERTS), ALU.mult), t, 3)

            def route_count(t):
                step(v.tensor_reduce(al_max[:], actor_log[:, t, :, :], AX.X, ALU.max), t, 4)
                step(v.tensor_tensor(al_less[:], actor_log[:, t, :, :], over(al_max[:], KMAX), ALU.is_lt), t, 5)
                step(v.scalar_tensor_tensor(al_cand[:], al_less[:], float(EXPERTS),
                                            iota_sb[:].unsqueeze(1).broadcast_to([P, BB, KMAX]), ALU.mult, ALU.add), t, 6)
                step(v.tensor_reduce(k_less1[:], al_cand[:], AX.X, ALU.min), t, 7)

            def route_rank(t):
                shape = [P, BB, EXPERTS, EXPERTS]
                mine = prob[:].unsqueeze(3).broadcast_to(shape)
                other = prob[:].unsqueeze(2).broadcast_to(shape)
                step(v.tensor_tensor(beats[:], other, mine, ALU.is_gt), t, 8)
                step(v.tensor_tensor(ties[:], other, mine, ALU.is_equal), t, 9)
                step(v.tensor_tensor(ties_lo[:], ties[:], tri_sb[:].unsqueeze(1).broadcast_to(shape), ALU.mult), t, 10)
                step(v.tensor_tensor(ahead[:], beats[:], ties_lo[:], ALU.add), t, 11)
                step(v.tensor_reduce(rank[:], ahead[:], AX.X, ALU.add), t, 12)

            def route_scores(t):
                step(v.tensor_tensor(chosen[:], rank[:], over(k_less1[:], EXPERTS), ALU.is_le), t, 13)
                step(v.tensor_tensor(score[:], prob[:], chosen[:], ALU.mult), t, 14)
                wait(dve, st_done, t)
                step(v.tensor_scalar(score16[:, :, 0:EXPERTS], score[:], S_SCALE, None, ALU.mult), t, 15)
                step(v.scalar_tensor_tensor(score16[:, :, EXPERTS:], score[:], S_SCALE, score16[:, :, 0:EXPERTS],
                                            ALU.mult, ALU.subtract), t, 16)

            def result(t, par):
                dve.wait_ge(yt_done, t + 1)
                if not isinstance(t, int) or t >= 2:
                    dve.wait_ge(stored[par], 8 * (t - par))
                v.tensor_tensor(out_sb[par], bank[7][:].rearrange("p (b d) -> p b d", b=BB), x2_all[:, t, :, :],
                                ALU.add).then_inc(out_ready, 1)

            def low_part(i, p):
                tile = PAIR * i + p
                dve.wait_ge(hid_hi_ready, tile + 1)
                v.tensor_tensor(hid_lo[p % HRING][:], hid[p % RING], hid_hi[p % HRING][:], ALU.subtract)\
                    .then_inc(hid_lo_ready, 1)

            def pair(i, first):
                last_pair = isinstance(i, int) and i == BLOCKS // 2 - 1
                for p in range(PAIR):
                    par, j = divmod(p, TILES)
                    t = 2 * i + par
                    tile = PAIR * i + p
                    if p >= 2 or not first:
                        low_part(i, p - 2)
                    dve.wait_ge(weighted_ready, tile + 1)
                    dve.wait_ge(up_done, tile + 1)
                    wait(dve, hid_lo_ready, tile - RING + 1)
                    v.scalar_tensor_tensor(hid[p % RING], bank[2 + p % U_BANKS][:], h_scale[:], weighted[p % RING],
                                           ALU.mult, ALU.mult).then_inc(hid_ready, 1)
                    if not (par == 1 and last_pair):
                        if j == 2:
                            route_probs(t + 1)
                        if j == 4:
                            route_count(t + 1)
                        if j == 6:
                            route_rank(t + 1)
                        if j == 8:
                            route_scores(t + 1)
                    if j == 19 and not (first and par == 0):
                        result(t - 1, 1 - par)

            dve.wait_ge(rexp_ready, 1)
            route_probs(0)
            route_count(0)
            route_rank(0)
            route_scores(0)
            pair(0, True)
            with dve.Fori(1, BLOCKS // 2 - 1) as i:
                pair(i, False)
            pair(BLOCKS // 2 - 1, False)
            for p in range(PAIR - 2, PAIR):
                low_part(BLOCKS // 2 - 1, p)
            result(BLOCKS - 1, 1)


def kernel(x, ctx_1024, L0_xattn_Wq, L0_xattn_bq, L0_xattn_Wk, L0_xattn_bk, L0_xattn_Wv, L0_xattn_bv,
           L0_ffn_router_w, L0_ffn_actor_w1, L0_ffn_actor_b1, L0_ffn_actor_w2, L0_ffn_actor_b2,
           L0_ffn_gate_w, L0_ffn_up_w, L0_ffn_down_w):
    import concourse.bacc as bacc
    from concourse.bass_utils import run_bass_kernel_spmd

    def units(w):
        w = np.asarray(w).reshape(EXPERTS, TILES, ROWS, P)
        return w.transpose(3, 1, 0, 2).reshape(P, TILES * P)

    down = np.asarray(L0_ffn_down_w).reshape(EXPERTS, P, TILES, ROWS).transpose(0, 3, 2, 1).reshape(P, TILES * P)
    pcols = np.zeros((P, 3), np.float32)
    pcols[:, 0] = L0_xattn_bq
    pcols[:, 1] = L0_xattn_bk
    pcols[:ACTOR, 2] = L0_ffn_actor_b1
    col = np.arange(P)
    arrays = {
        "x": np.asarray(x).reshape(BATCHES * P, P),
        "ctx_t": np.asarray(ctx_1024).reshape(BATCHES * CTX, P).T,
        "wcols": np.concatenate([np.asarray(w).T for w in (L0_xattn_Wq, L0_xattn_Wk, L0_xattn_Wv, L0_ffn_router_w,
                                                           L0_ffn_actor_w1)], axis=1),
        "pcols": pcols,
        "bv": np.asarray(L0_xattn_bv),
        "b2": np.asarray(L0_ffn_actor_b2),
        "w2t": np.asarray(L0_ffn_actor_w2).T,
        "gate_t": units(L0_ffn_gate_w),
        "up_t": units(L0_ffn_up_w),
        "down_t": down,
        "ident": np.eye(P, dtype=np.float32),
        "ident16": np.eye(P, dtype=np.float16),
        "sel": (np.arange(2 * EXPERTS)[:, None] % EXPERTS == col[None, :] // ROWS).astype(np.float16),
        "tri": np.broadcast_to(np.tri(EXPERTS, k=-1, dtype=np.float32), (P, EXPERTS, EXPERTS)),
        "iota": np.broadcast_to(np.arange(KMAX, dtype=np.float32), (P, KMAX)),
    }
    arrays = {n: np.ascontiguousarray(a) for n, a in arrays.items()}
    nc = bacc.Bacc("TRN2", target_bir_lowering=False, num_devices=1)
    args = [nc.dram_tensor(f"in_{n}", a.shape, mybir.dt.from_np(a.dtype), kind="ExternalInput").ap()
            for n, a in arrays.items()]
    args.append(nc.dram_tensor("out", (BATCHES * P, P), F32, kind="ExternalOutput").ap())
    program(nc, *args)
    r = run_bass_kernel_spmd(nc, [{f"in_{n}": a for n, a in arrays.items()}], core_ids=[0])
    return r.results[0]["out"].reshape(BATCHES, P, P)
```

```python
from contextlib import ExitStack

import numpy as np

import concourse.bass as bass
from concourse import mybir

F32 = mybir.dt.float32
F16 = mybir.dt.float16
U32 = mybir.dt.uint32
ALU = mybir.AluOpType
ACT = mybir.ActivationFunctionType
AX = mybir.AxisListType

P = 128
BATCHES, CTX = 64, 120
BB = 4
NT = BB * P
NC = BB * CTX
BLOCKS = BATCHES // BB
EXPERTS, HIDDEN = 8, 336
ROWS = P // EXPERTS
TILES = HIDDEN // ROWS
ACTOR, KMAX = 50, 6
EPS = 1e-5
GELU_C, GELU_A = 0.7978845608028654, 0.044715
SCALE = float(P) ** -0.5

G_BANKS, U_BANKS = 2, 3
RING, HRING = 3, 6
DOWN_LAG = 4
PAIR = 2 * TILES

W_TOP = 256.0
H_SCALE = 2.0 ** -7
S_SCALE = 256.0

ROUTE_STEPS = 16


def program(nc, x, ctx_t, wcols, pcols, bv, b2, w2t, gate_t, up_t, down_t, ident, ident16, sel, tri, iota, out):
    x_blocks = x.rearrange("(t b p) d -> t p b d", b=BB, p=P)
    out_blocks = out.rearrange("(t b p) d -> t p b d", b=BB, p=P)
    ctx_blocks = ctx_t.rearrange("p (t n) -> t p n", n=NC)

    with ExitStack() as stack:
        def sb(name, shape, dt=F32):
            return stack.enter_context(nc.sbuf_tensor(name, shape, dt))

        def sem(name):
            return stack.enter_context(nc.semaphore(name))

        bank = [stack.enter_context(nc.psum_tensor(f"bank{k}", [P, 512], F32)) for k in range(8)]

        wcol_sb = sb("wcol_sb", [P, 3 * P + EXPERTS + ACTOR])
        wq_t, wk_t, wv_t = (wcol_sb[:, k * P:(k + 1) * P] for k in range(3))
        router_t = wcol_sb[:, 3 * P:3 * P + EXPERTS]
        w1_t = wcol_sb[:, 3 * P + EXPERTS:]
        pcol_sb = sb("pcol_sb", [P, 3])
        bq_scaled = sb("bq_scaled", [P, 1])
        bv_sb = sb("bv_sb", [P, P])
        b2_sb = sb("b2_sb", [P, KMAX])
        w2_sb = sb("w2_sb", [ACTOR, KMAX])
        ident_sb = sb("ident_sb", [P, P])
        ident16_sb = sb("ident16_sb", [P, P], F16)
        sel_sb = sb("sel_sb", [2 * EXPERTS, P], F16)
        tri_sb = sb("tri_sb", [P, EXPERTS, EXPERTS])
        iota_sb = sb("iota_sb", [P, KMAX])
        eps_sb = sb("eps_sb", [P, BB])
        neg_half = sb("neg_half", [P, BB])
        work = sb("work", [P, 2 * TILES * P])
        raw = [work[:, 0:TILES * P], work[:, TILES * P:], sb("raw_down", [P, TILES * P])[:]]
        w_hi = [sb(f"{n}_hi", [P, TILES * P], F16) for n in ("gate", "up", "down")]
        w_lo = [sb(f"{n}_lo", [P, TILES * P], F16) for n in ("gate", "up", "down")]
        w_abs = sb("w_abs", [P, 3])
        w_top = sb("w_top", [P, 3])
        w_pow = sb("w_pow", [P, 3])
        w_inv = sb("w_inv", [P, 3])
        w_mul = sb("w_mul", [P, 3])
        silu_scale = sb("silu_scale", [P, 1])
        h_scale = sb("h_scale", [P, 1])
        y_scale = sb("y_scale", [P, 2])

        x2_all = sb("x2_all", [P, BLOCKS, BB, P])
        xn_hi = sb("xn_hi", [P, BLOCKS, NT], F16)
        xn_lo = sb("xn_lo", [P, BLOCKS, NT], F16)
        route_exp = sb("route_exp", [P, BLOCKS, BB, EXPERTS])
        actor_log = sb("actor_log", [P, BLOCKS, BB, KMAX])

        x_in = [sb(f"x_in{k}", [P, BB, P]) for k in range(2)]
        ctx_in = [sb(f"ctx_in{k}", [P, NC]) for k in range(2)]
        stats1 = sb("stats1", [P, BB, 6])
        mv1 = [sb(f"mv1_{k}", [P, BB, 2]) for k in range(2)]
        ve1 = sb("ve1", [P, BB])
        rstd1 = sb("rstd1", [P, BB])
        xn_nat = [sb(f"xn_nat{k}", [P, BB, P]) for k in range(2)]
        xn_t = sb("xn_t", [P, NT])
        q_t = sb("q_t", [P, NT])
        k_t = sb("k_t", [P, NC])
        v_sb = [sb(f"v_sb{k}", [CTX, BB * P]) for k in range(2)]
        neg_max = [sb(f"neg_max{k}", [P, BB]) for k in range(2)]
        probs = sb("probs", [P, BB, CTX])
        sums = [sb(f"sums{k}", [P, BB]) for k in range(2)]
        inv_sum = sb("inv_sum", [P, BB])
        probs_t = sb("probs_t", [CTX, BB * P])
        stats2 = sb("stats2", [P, BB, 6])
        mv2 = [sb(f"mv2_{k}", [P, BB, 2]) for k in range(2)]
        ve2 = sb("ve2", [P, BB])
        rstd2 = [sb(f"rstd2_{k}", [P, BB]) for k in range(2)]
        xn2_nat = [sb(f"xn2_nat{k}", [P, BB, P]) for k in range(2)]
        xn2_t = sb("xn2_t", [P, NT])
        route_max = sb("route_max", [P, BB])
        a_sb = [sb(f"a_sb{k}", [ACTOR, NT]) for k in range(2)]
        shared = [sb(f"shared{k}", [P, NT]) for k in range(5)]
        a_sq, a_poly, a_arg, a_tanh, a_gelu2 = (buf[0:ACTOR, :] for buf in shared)
        al_raw = sb("al_raw", [P, BB, KMAX])

        silu, weighted, hid = ([work[:, (r * RING + k) * NT:(r * RING + k + 1) * NT] for k in range(RING)]
                               for r in range(3))
        hid_hi = [sb(f"hid_hi{k}", [P, NT], F16) for k in range(HRING)]
        hid_lo = [sb(f"hid_lo{k}", [P, NT], F16) for k in range(HRING)]
        p_sum = sb("p_sum", [P, BB])
        p_inv = sb("p_inv", [P, BB])
        prob = sb("prob", [P, BB, EXPERTS])
        al_max = sb("al_max", [P, BB])
        al_less = sb("al_less", [P, BB, KMAX])
        al_cand = sb("al_cand", [P, BB, KMAX])
        k_less1 = sb("k_less1", [P, BB])
        beats = sb("beats", [P, BB, EXPERTS, EXPERTS])
        ties = sb("ties", [P, BB, EXPERTS, EXPERTS])
        ties_lo = sb("ties_lo", [P, BB, EXPERTS, EXPERTS])
        ahead = sb("ahead", [P, BB, EXPERTS, EXPERTS])
        rank = sb("rank", [P, BB, EXPERTS])
        chosen = sb("chosen", [P, BB, EXPERTS])
        score = sb("score", [P, BB, EXPERTS])
        score16 = sb("score16", [P, BB, 2 * EXPERTS], F16)
        score_t = sb("score_t", [2 * EXPERTS, NT], F16)
        score_bc = [shared[k][:] for k in range(2)]
        y_sb = shared[2][:]
        out_sb = [shared[3 + k][:].rearrange("p (b d) -> p b d", b=BB) for k in range(2)]

        consts_in = sem("consts_in")
        weights_in = [sem(f"weights_in{k}") for k in range(3)]
        x_loaded = [sem(f"x_loaded{k}") for k in range(2)]
        ctx_loaded = [sem(f"ctx_loaded{k}") for k in range(2)]
        setup_vec = sem("setup_vec")
        setup_pool = sem("setup_pool")
        w_stat = sem("w_stat")
        w_all = sem("w_all")
        w_chain = sem("w_chain")
        w_hi_done = sem("w_hi_done")
        w_split = sem("w_split")
        ln1_stats, ln1_mv, ln1_ve, ln1_rstd, xn_ready, xb_ready = (
            sem(n) for n in ("ln1_stats", "ln1_mv", "ln1_ve", "ln1_rstd", "xn_ready", "xb_ready"))
        t1_done, xnt_ready, kp_done, kt_ready, vp_done, v_ready, qp_done, qt_ready = (
            sem(n) for n in ("t1_done", "xnt_ready", "kp_done", "kt_ready", "vp_done", "v_ready", "qp_done",
                             "qt_ready"))
        e_done, max_ready, exp_done, pt_done, ptt_ready, o_done, inv_ready, x2_ready = (
            sem(n) for n in ("e_done", "max_ready", "exp_done", "pt_done", "ptt_ready", "o_done", "inv_ready",
                             "x2_ready"))
        ln2_stats, ln2_mv, ln2_ve, ln2_rstd, xn2_ready, t2_done, xn2t_ready, hi_ready, lo_ready = (
            sem(n) for n in ("ln2_stats", "ln2_mv", "ln2_ve", "ln2_rstd", "xn2_ready", "t2_done", "xn2t_ready",
                             "hi_ready", "lo_ready"))
        ah_done, a_ready, sq_ready, poly_ready, arg_ready, tanh_ready, gelu_ready, al_done, al_add, al_ready = (
            sem(n) for n in ("ah_done", "a_ready", "sq_ready", "poly_ready", "arg_ready", "tanh_ready",
                             "gelu_ready", "al_done", "al_add", "al_ready"))
        r_done, rmax_ready, rsub_ready, rexp_ready = (
            sem(n) for n in ("r_done", "rmax_ready", "rsub_ready", "rexp_ready"))
        gate_done, up_done, silu_ready, weighted_ready, hid_ready, hid_hi_ready, hid_lo_ready, down_done = (
            sem(n) for n in ("gate_done", "up_done", "silu_ready", "weighted_ready", "hid_ready", "hid_hi_ready",
                             "hid_lo_ready", "down_done"))
        route_step, st_done, st_ready, bc_done, bc_ready, y_ready, yt_done, out_ready = (
            sem(n) for n in ("route_step", "st_done", "st_ready", "bc_done", "bc_ready", "y_ready", "yt_done",
                             "out_ready"))
        stored = [sem(f"stored{k}") for k in range(2)]

        N_CONSTS = 11

        def wait(eng, s, value):
            if not isinstance(value, int) or value > 0:
                eng.wait_ge(s, value)

        def live(slot, lag):
            return not isinstance(slot, int) or 0 <= slot - lag < BLOCKS

        def slots(eng, body):
            for s in range(-1, 4):
                body(s, s % 2)
            with eng.Fori(2, BLOCKS // 2 - 1) as i:
                body(2 * i, 0)
                body(2 * i + 1, 1)
            for s in range(BLOCKS - 2, BLOCKS + 4):
                body(s, s % 2)

        block = stack.enter_context(nc.Block())

        @block.sync
        def _(sp):
            for dst, src in ((wcol_sb[:], wcols), (pcol_sb[:], pcols), (ident_sb[:], ident),
                             (bv_sb[:], bv.partition_broadcast(P)), (b2_sb[:], b2.partition_broadcast(P)),
                             (w2_sb[:], w2t), (ident16_sb[:], ident16), (sel_sb[:], sel),
                             (tri_sb[:], tri), (iota_sb[:], iota)):
                sp.dma_start(dst, src).then_inc(consts_in, 16)

            def loads(b, par, n):
                wait(sp, xb_ready, b - 1)
                wait(sp, xn_ready, b - 1)
                sp.dma_start(x_in[par][:], x_blocks[b]).then_inc(x_loaded[par], 16)
                wait(sp, vp_done, b - 1)
                sp.dma_start(ctx_in[par][:], ctx_blocks[b]).then_inc(ctx_loaded[par], 16)

            loads(0, 0, 0)
            loads(1, 1, 0)
            for k, w in enumerate((gate_t, up_t, down_t)):
                sp.dma_start(raw[k], w).then_inc(weights_in[k], 16)
            with sp.Fori(1, BLOCKS // 2) as i:
                loads(2 * i, 0, i)
                loads(2 * i + 1, 1, i)

            with sp.Fori(0, BLOCKS // 2) as i:
                for par in range(2):
                    sp.wait_ge(out_ready, 2 * i + par + 1)
                    sp.dma_start(out_blocks[2 * i + par], out_sb[par]).then_inc(stored[par], 16)
            for par in range(2):
                sp.wait_ge(stored[par], 16 * (BLOCKS // 2))

        @block.tensor
        def _(pe):
            mm = nc.tensor.matmul

            def upto(s, lag):
                return min(s - lag + 1, BLOCKS) if isinstance(s, int) else s - lag + 1

            def slot(s, par):
                if live(s, 1):
                    pe.wait_ge(qt_ready, s)
                    wait(pe, exp_done, BB * (s - 1))
                    for b in range(BB):
                        last = mm(bank[4][:, b * CTX:(b + 1) * CTX], q_t[:, b * P:(b + 1) * P],
                                  k_t[:, b * CTX:(b + 1) * CTX], start=True, stop=True)
                    last.then_inc(e_done, 1)
                if live(s, 2):
                    pe.wait_ge(ptt_ready, s - 1)
                    pe.wait_ge(v_ready, s - 1)
                    wait(pe, x2_ready, s - 2)
                    for b in range(BB):
                        last = mm(bank[6][:, b * P:(b + 1) * P], probs_t[:, b * P:(b + 1) * P],
                                  v_sb[par][:, b * P:(b + 1) * P], start=True, stop=True)
                    last.then_inc(o_done, 1)
                if live(s, 0):
                    pe.wait_ge(xn_ready, s + 1)
                    wait(pe, xn2t_ready, s - 3)
                    for b in range(BB):
                        last = nc.tensor.transpose(bank[0][:, b * P:(b + 1) * P], xn_nat[par][:, b, :], ident_sb[:])
                    last.then_inc(t1_done, 1)
                    pe.wait_ge(ctx_loaded[par], 8 * (s - par) + 16)
                    wait(pe, kt_ready, s)
                    wait(pe, rsub_ready, s - 3)
                    mm(bank[1][:, 0:NC], wk_t, ctx_in[par][:], start=True, stop=True).then_inc(kp_done, 1)
                    wait(pe, v_ready, s)
                    for b in range(BB):
                        last = mm(bank[2][0:CTX, b * P:(b + 1) * P], ctx_in[par][:, b * CTX:(b + 1) * CTX], wv_t,
                                  start=True, stop=True)
                    last.then_inc(vp_done, 1)
                if live(s, 3):
                    pe.wait_ge(xn2_ready, s - 2)
                    wait(pe, xnt_ready, upto(s, 0))
                    for b in range(BB):
                        last = nc.tensor.transpose(bank[0][:, b * P:(b + 1) * P], xn2_nat[1 - par][:, b, :], ident_sb[:])
                    last.then_inc(t2_done, 1)
                if live(s, 0):
                    pe.wait_ge(xnt_ready, s + 1)
                    wait(pe, qt_ready, s)
                    mm(bank[3][:], wq_t, xn_t[:], start=True, stop=True).then_inc(qp_done, 1)
                if live(s, 1):
                    pe.wait_ge(exp_done, BB * s)
                    wait(pe, ptt_ready, s - 1)
                    for b in range(BB):
                        last = nc.tensor.transpose(bank[5][0:CTX, b * P:(b + 1) * P], probs[:, b, :], ident_sb[:])
                    last.then_inc(pt_done, 1)
                if live(s, 3):
                    pe.wait_ge(xn2t_ready, s - 2)
                    wait(pe, kt_ready, upto(s, 0))
                    for b in range(BB):
                        last = mm(bank[1][:, NC + b * EXPERTS:NC + (b + 1) * EXPERTS], xn2_t[:, b * P:(b + 1) * P],
                                  router_t, start=True, stop=True)
                    last.then_inc(r_done, 1)
                if live(s, 4):
                    pe.wait_ge(gelu_ready, s - 3)
                    for b in range(BB):
                        last = mm(bank[7][:, b * KMAX:(b + 1) * KMAX], a_gelu2[:, b * P:(b + 1) * P], w2_sb[:],
                                  start=True, stop=True)
                    last.then_inc(al_done, 1)
                if live(s, 3):
                    wait(pe, al_add, s - 3)
                    mm(bank[7][0:ACTOR, :], w1_t, xn2_t[:], start=True, stop=True).then_inc(ah_done, 1)

            pe.wait_ge(consts_in, 16 * (N_CONSTS - 1))
            slots(pe, slot)

            def score_transposes(t):
                pe.wait_ge(route_step, ROUTE_STEPS * (t + 1))
                wait(pe, out_ready, t - 2)
                for b in range(BB):
                    last = nc.tensor.transpose(bank[7][0:2 * EXPERTS, :].bitcast(F16)[:, b * P:(b + 1) * P],
                                               score16[:, b, :], ident16_sb[:])
                last.then_inc(st_done, 1)

            def score_broadcast(t):
                pe.wait_ge(st_ready, t + 1)
                mm(bank[7][:], sel_sb[:], score_t[:], start=True, stop=True).then_inc(bc_done, 1)

            def result_transposes(t):
                pe.wait_ge(y_ready, t + 1)
                wait(pe, bc_ready, t + 3 if not isinstance(t, int) else min(t + 3, BLOCKS))
                for b in range(BB):
                    last = nc.tensor.transpose(bank[7][:, b * P:(b + 1) * P], y_sb[:, b * P:(b + 1) * P], ident_sb[:])
                last.then_inc(yt_done, 1)

            def split_product(dst, w, tile, hi, lo, start, stop):
                cols = slice(tile * P, (tile + 1) * P)
                mm(dst, w_hi[w][:, cols], lo, start=start, stop=False)
                mm(dst, w_lo[w][:, cols], hi, start=False, stop=False)
                return mm(dst, w_hi[w][:, cols], hi, start=False, stop=stop)

            def down(i, p):
                j, par = p % TILES, (p // TILES) % 2
                tile = PAIR * i + p
                pe.wait_ge(hid_lo_ready, tile + 1)
                if j == 0:
                    wait(pe, y_ready, 2 * i + par - 1)
                split_product(bank[5 + par][:], 2, j, hid_hi[p % HRING][:], hid_lo[p % HRING][:],
                              j == 0, j == TILES - 1).then_inc(down_done, 1)

            def pair(i, first):
                for p in range(PAIR):
                    par, j = divmod(p, TILES)
                    t = 2 * i + par
                    tile = PAIR * i + p
                    wait(pe, silu_ready, tile - G_BANKS + 1)
                    split_product(bank[p % G_BANKS][:], 0, j, xn_hi[:, t, :], xn_lo[:, t, :], True, True)\
                        .then_inc(gate_done, 1)
                    wait(pe, hid_ready, tile - U_BANKS + 1)
                    split_product(bank[2 + p % U_BANKS][:], 1, j, xn_hi[:, t, :], xn_lo[:, t, :], True, True)\
                        .then_inc(up_done, 1)
                    if p >= DOWN_LAG or not first:
                        down(i, p - DOWN_LAG)
                    if j == 12 and not (par == 1 and isinstance(i, int) and i == BLOCKS // 2 - 1):
                        score_transposes(t + 1)
                    if j == 14 and not (par == 1 and isinstance(i, int) and i == BLOCKS // 2 - 1):
                        score_broadcast(t + 1)
                    if j == 18 and not (first and par == 0):
                        result_transposes(t - 1)

            pe.wait_ge(w_split, 5)
            pe.wait_ge(lo_ready, BLOCKS)
            pe.wait_ge(hi_ready, BLOCKS)
            pe.wait_ge(al_ready, BLOCKS)
            pe.wait_ge(rsub_ready, BLOCKS)
            pe.wait_ge(x2_ready, BLOCKS)
            score_transposes(0)
            score_broadcast(0)
            pe.wait_ge(bc_ready, 1)
            pair(0, True)
            with pe.Fori(1, BLOCKS // 2 - 1) as i:
                pair(i, False)
            pair(BLOCKS // 2 - 1, False)
            for p in range(PAIR - DOWN_LAG, PAIR):
                down(BLOCKS // 2 - 1, p)
            result_transposes(BLOCKS - 1)

        @block.scalar
        def _(act):
            af = nc.scalar.activation

            def slot(s, par):
                if live(s, 1):
                    pe_prev = 1 - par
                    act.wait_ge(max_ready, s)
                    wait(act, pt_done, s - 1)
                    wait(act, inv_ready, s - 2)
                    for b in range(BB):
                        af(probs[:, b, :], bank[4][:, b * CTX:(b + 1) * CTX], ACT.Exp, bias=neg_max[pe_prev][:, b:b + 1],
                           accum_out=sums[pe_prev][:, b:b + 1]).then_inc(exp_done, 1)
                if live(s, 0):
                    act.wait_ge(t1_done, s + 1)
                    wait(act, qp_done, s)
                    af(xn_t[:], bank[0][:], ACT.Copy).then_inc(xnt_ready, 1)
                    act.wait_ge(kp_done, s + 1)
                    wait(act, e_done, s)
                    af(k_t[:], bank[1][:, 0:NC], ACT.Identity, bias=pcol_sb[:, 1:2]).then_inc(kt_ready, 1)
                if live(s, 4):
                    act.wait_ge(arg_ready, s - 3)
                    wait(act, gelu_ready, s - 4)
                    af(a_tanh, a_arg, ACT.Tanh, scale=GELU_C).then_inc(tanh_ready, 1)
                if live(s, 3):
                    act.wait_ge(t2_done, s - 2)
                    wait(act, ah_done, s - 3)
                    wait(act, hi_ready, s - 3)
                    wait(act, lo_ready, s - 3)
                    af(xn2_t[:], bank[0][:], ACT.Copy).then_inc(xn2t_ready, 1)
                if live(s, 0):
                    act.wait_ge(qp_done, s + 1)
                    af(q_t[:], bank[3][:], ACT.Identity, bias=bq_scaled[:], scale=SCALE).then_inc(qt_ready, 1)
                if live(s, 4):
                    act.wait_ge(rsub_ready, s - 3)
                    af(route_exp[:, s - 4, :, :], route_exp[:, s - 4, :, :], ACT.Exp).then_inc(rexp_ready, 1)
                if live(s, 1):
                    act.wait_ge(pt_done, s)
                    wait(act, o_done, s - 1)
                    af(probs_t[:], bank[5][0:CTX, :], ACT.Copy).then_inc(ptt_ready, 1)
                if live(s, 3):
                    act.wait_ge(ah_done, s - 2)
                    wait(act, gelu_ready, s - 4)
                    af(a_sb[1 - par][:], bank[7][0:ACTOR, :], ACT.Identity, bias=pcol_sb[0:ACTOR, 2:3])\
                        .then_inc(a_ready, 1)
                    act.wait_ge(a_ready, s - 2)
                    wait(act, poly_ready, s - 3)
                    af(a_sq, a_sb[1 - par][:], ACT.Square, scale=GELU_A ** 0.5).then_inc(sq_ready, 1)

            act.wait_ge(consts_in, 16 * (N_CONSTS - 1))
            act.wait_ge(setup_vec, 2)
            nc.scalar.preload_act_table(ACT.Exp)
            slots(act, slot)
            act.wait_ge(w_chain, 4)

            def score_copy(t):
                act.wait_ge(st_done, t + 1)
                wait(act, bc_done, t)
                af(score_t[:], bank[7][0:2 * EXPERTS, :].bitcast(F16)[:, 0:NT], ACT.Copy).then_inc(st_ready, 1)

            def score_spread(t, par):
                act.wait_ge(bc_done, t + 1)
                wait(act, weighted_ready, TILES * (t - 1))
                af(score_bc[par], bank[7][:], ACT.Copy, scale=1.0 / S_SCALE).then_inc(bc_ready, 1)

            def result_copy(t, par):
                act.wait_ge(down_done, TILES * (t + 1))
                wait(act, yt_done, t)
                af(y_sb, bank[5 + par][:], ACT.Copy, scale=y_scale[:, 1:2]).then_inc(y_ready, 1)

            def high_part(i, p):
                tile = PAIR * i + p
                act.wait_ge(hid_ready, tile + 1)
                wait(act, down_done, tile - HRING + 1)
                af(hid_hi[p % HRING][:], hid[p % RING], ACT.Copy).then_inc(hid_hi_ready, 1)

            def pair(i, first):
                for p in range(PAIR):
                    par, j = divmod(p, TILES)
                    t = 2 * i + par
                    tile = PAIR * i + p
                    act.wait_ge(gate_done, tile + 1)
                    wait(act, weighted_ready, tile - RING + 1)
                    af(silu[p % RING], bank[p % G_BANKS][:], ACT.Silu, scale=silu_scale[:]).then_inc(silu_ready, 1)
                    if p >= 2 or not first:
                        high_part(i, p - 2)
                    if j == 12 and not (par == 1 and isinstance(i, int) and i == BLOCKS // 2 - 1):
                        score_copy(t + 1)
                    if j == 14 and not (par == 1 and isinstance(i, int) and i == BLOCKS // 2 - 1):
                        score_spread(t + 1, 1 - par)
                    if j == DOWN_LAG + 1 and not (first and par == 0):
                        result_copy(t - 1, 1 - par)

            nc.scalar.preload_act_table(ACT.Silu)
            score_copy(0)
            score_spread(0, 0)
            pair(0, True)
            with act.Fori(1, BLOCKS // 2 - 1) as i:
                pair(i, False)
            pair(BLOCKS // 2 - 1, False)
            for p in range(PAIR - 2, PAIR):
                high_part(BLOCKS // 2 - 1, p)
            result_copy(BLOCKS - 1, 1)

        @block.gpsimd
        def _(pool):
            g = nc.gpsimd
            g.memset(eps_sb[:], EPS).then_inc(setup_pool, 1)
            g.memset(neg_half[:], -0.5).then_inc(setup_pool, 1)
            pool.wait_ge(setup_pool, 2)
            pool.wait_ge(consts_in, 16 * (N_CONSTS - 1))

            def slot(s, par):
                nxt = 1 - par
                if live(s, 4):
                    pool.wait_ge(sq_ready, s - 3)
                    wait(pool, arg_ready, s - 4)
                    g.tensor_tensor(a_poly, a_sq, a_sb[par][:], ALU.mult).then_inc(poly_ready, 1)
                    pool.wait_ge(poly_ready, s - 3)
                    wait(pool, tanh_ready, s - 4)
                    g.tensor_tensor(a_arg, a_poly, a_sb[par][:], ALU.add).then_inc(arg_ready, 1)
                if live(s, -1):
                    pool.wait_ge(ln1_mv, s + 2)
                    wait(pool, ln1_rstd, s + 1)
                    g.tensor_tensor(ve1[:], mv1[nxt][:, :, 1], eps_sb[:], ALU.add).then_inc(ln1_ve, 1)
                    pool.wait_ge(ln1_ve, s + 2)
                    wait(pool, xn_ready, s + 1)
                    g.tensor_tensor(rstd1[:], ve1[:], neg_half[:], ALU.pow).then_inc(ln1_rstd, 1)
                if live(s, 2):
                    pool.wait_ge(ln2_mv, s - 1)
                    wait(pool, ln2_rstd, s - 2)
                    g.tensor_tensor(ve2[:], mv2[par][:, :, 1], eps_sb[:], ALU.add).then_inc(ln2_ve, 1)
                    pool.wait_ge(ln2_ve, s - 1)
                    wait(pool, xn2_ready, s - 3)
                    g.tensor_tensor(rstd2[par][:], ve2[:], neg_half[:], ALU.pow).then_inc(ln2_rstd, 1)
                if live(s, -1):
                    g.tensor_tensor(x2_all[:, s + 1, :, :], x_in[nxt][:],
                                    bv_sb[:].unsqueeze(1).broadcast_to([P, BB, P]), ALU.add).then_inc(xb_ready, 1)
                if live(s, 3):
                    pool.wait_ge(hi_ready, s - 2)
                    g.tensor_tensor(xn_lo[:, s - 3, :], xn2_t[:], xn_hi[:, s - 3, :], ALU.subtract).then_inc(lo_ready, 1)
                if isinstance(s, int) and s == 3:
                    pool.wait_ge(w_stat, 3)
                    g.partition_all_reduce(w_top[:], w_abs[:], P, bass.bass_isa.ReduceOp.max).then_inc(w_all, 1)

            slots(pool, slot)

            with pool.Fori(0, BLOCKS // 2) as i:
                for p in range(PAIR):
                    par, j = divmod(p, TILES)
                    tile = PAIR * i + p
                    if j == 0:
                        pool.wait_ge(bc_ready, 2 * i + par + 1)
                    pool.wait_ge(silu_ready, tile + 1)
                    pool.wait_ge(up_done, tile + 1)
                    g.tensor_tensor(weighted[p % RING], silu[p % RING], score_bc[par], ALU.mult)\
                        .then_inc(weighted_ready, 1)

        @block.vector
        def _(dve):
            v = nc.vector

            def weight_magnitude(k):
                dve.wait_ge(weights_in[k], 16)
                v.tensor_reduce(w_abs[:, k:k + 1], raw[k], AX.X, ALU.max, apply_absolute_value=True)\
                    .then_inc(w_stat, 1)

            def weight_scales():
                dve.wait_ge(w_all, 1)
                v.tensor_scalar(w_pow[:], w_top[:], 1e-30, None, ALU.max).then_inc(w_chain, 1)
                dve.wait_ge(w_chain, 1)
                v.tensor_scalar(w_pow[:].bitcast(U32), w_pow[:].bitcast(U32), 0x7F800000, None, ALU.bitwise_and)\
                    .then_inc(w_chain, 1)
                dve.wait_ge(w_chain, 2)
                v.reciprocal(w_inv[:], w_pow[:]).then_inc(w_chain, 1)
                dve.wait_ge(w_chain, 3)
                v.tensor_scalar(w_mul[:], w_inv[:], W_TOP / 2, None, ALU.mult).then_inc(w_split, 1)
                v.tensor_scalar(silu_scale[:], w_pow[:, 0:1], 2 / W_TOP, None, ALU.mult)
                v.tensor_scalar(h_scale[:], w_inv[:, 0:1], H_SCALE / 2, None, ALU.mult)
                v.tensor_tensor(y_scale[:, 0:1], w_pow[:, 0:1], w_pow[:, 1:2], ALU.mult).then_inc(w_split, 1)
                dve.wait_ge(w_split, 2)
                v.tensor_scalar(y_scale[:, 1:2], y_scale[:, 0:1], w_pow[:, 2:3], 8.0 / (W_TOP * W_TOP * H_SCALE),
                                ALU.mult, ALU.mult).then_inc(w_chain, 1)

            def weight_parts(k):
                v.tensor_scalar(w_hi[k][:], raw[k], w_mul[:, k:k + 1], None, ALU.mult).then_inc(w_hi_done, 1)
                dve.wait_ge(w_hi_done, k + 1)
                v.scalar_tensor_tensor(w_lo[k][:], raw[k], w_mul[:, k:k + 1], w_hi[k][:], ALU.mult, ALU.subtract)\
                    .then_inc(w_split, 1)

            def slot(s, par):
                nxt = 1 - par
                if live(s, 1):
                    dve.wait_ge(e_done, s)
                    wait(dve, exp_done, BB * (s - 2))
                    v.tensor_reduce(neg_max[nxt][:], bank[4][:, 0:NC].rearrange("p (b n) -> p b n", b=BB), AX.X,
                                    ALU.max, negate=True).then_inc(max_ready, 1)
                if live(s, 2):
                    wait(dve, x2_ready, s - 2)
                    v.reciprocal(inv_sum[:], sums[par][:]).then_inc(inv_ready, 1)
                    dve.wait_ge(o_done, s - 1)
                    dve.wait_ge(xb_ready, s - 1)
                    dve.wait_ge(inv_ready, s - 1)
                    for b in range(BB):
                        last = v.scalar_tensor_tensor(x2_all[:, s - 2, b, :], bank[6][:, b * P:(b + 1) * P],
                                                      inv_sum[:, b:b + 1], x2_all[:, s - 2, b, :], ALU.mult, ALU.add)
                    last.then_inc(x2_ready, 1)
                if live(s, -1):
                    wait(dve, ln1_mv, s + 1)
                    dve.wait_ge(x_loaded[nxt], 8 * (s + 1 - nxt) + 16)
                    for b in range(BB):
                        last = v.bn_stats(stats1[:, b, :], x_in[nxt][:, b, :])
                    last.then_inc(ln1_stats, 1)
                    dve.wait_ge(ln1_stats, s + 2)
                    wait(dve, xn_ready, s)
                if live(s, 2):
                    dve.wait_ge(x2_ready, s - 1)
                    wait(dve, ln2_mv, s - 2)
                if live(s, 0):
                    dve.wait_ge(vp_done, s + 1)
                    wait(dve, o_done, s - 1)
                    v.tensor_copy(v_sb[par][:], bank[2][0:CTX, :]).then_inc(v_ready, 1)
                if live(s, 4):
                    dve.wait_ge(tanh_ready, s - 3)
                    wait(dve, al_done, s - 4)
                    v.scalar_tensor_tensor(a_gelu2, a_tanh, 1.0, a_sb[par][:], ALU.add, ALU.mult)\
                        .then_inc(gelu_ready, 1)
                if live(s, -1):
                    for b in range(BB):
                        last = v.bn_aggr(mv1[nxt][:, b, :], stats1[:, b, :])
                    last.then_inc(ln1_mv, 1)
                if live(s, 2):
                    for b in range(BB):
                        last = v.bn_stats(stats2[:, b, :], x2_all[:, s - 2, b, :])
                    last.then_inc(ln2_stats, 1)
                    dve.wait_ge(ln2_stats, s - 1)
                    wait(dve, xn2_ready, s - 3)
                if live(s, 3):
                    dve.wait_ge(xn2t_ready, s - 2)
                    v.tensor_copy(xn_hi[:, s - 3, :], xn2_t[:]).then_inc(hi_ready, 1)
                if live(s, 2):
                    for b in range(BB):
                        last = v.bn_aggr(mv2[par][:, b, :], stats2[:, b, :])
                    last.then_inc(ln2_mv, 1)
                if live(s, 3):
                    logits = bank[1][:, NC:NC + BB * EXPERTS].rearrange("p (b e) -> p b e", b=BB)
                    dve.wait_ge(r_done, s - 2)
                    wait(dve, rsub_ready, s - 3)
                    v.tensor_reduce(route_max[:], logits, AX.X, ALU.max).then_inc(rmax_ready, 1)
                    dve.wait_ge(rmax_ready, s - 2)
                    v.tensor_tensor(route_exp[:, s - 3, :, :], logits,
                                    route_max[:].unsqueeze(2).broadcast_to([P, BB, EXPERTS]), ALU.subtract)\
                        .then_inc(rsub_ready, 1)
                if live(s, 4):
                    dve.wait_ge(al_done, s - 3)
                    wait(dve, al_ready, s - 4)
                    v.scalar_tensor_tensor(al_raw[:], bank[7][:, 0:BB * KMAX].rearrange("p (b k) -> p b k", b=BB), 0.5,
                                           b2_sb[:].unsqueeze(1).broadcast_to([P, BB, KMAX]), ALU.mult, ALU.add)\
                        .then_inc(al_add, 1)
                    dve.wait_ge(al_add, s - 3)
                    v.tensor_scalar(actor_log[:, s - 4, :, :], al_raw[:], -30.0, 30.0, ALU.max, ALU.min)\
                        .then_inc(al_ready, 1)
                if live(s, -1):
                    dve.wait_ge(ln1_rstd, s + 2)
                    wait(dve, t1_done, s)
                    for b in range(BB):
                        last = v.tensor_scalar(xn_nat[nxt][:, b, :], x_in[nxt][:, b, :], mv1[nxt][:, b, 0:1],
                                               rstd1[:, b:b + 1], ALU.subtract, ALU.mult)
                    last.then_inc(xn_ready, 1)
                if live(s, 2):
                    dve.wait_ge(ln2_rstd, s - 1)
                    wait(dve, t2_done, s - 3)
                    for b in range(BB):
                        last = v.tensor_scalar(xn2_nat[par][:, b, :], x2_all[:, s - 2, b, :], mv2[par][:, b, 0:1],
                                               rstd2[par][:, b:b + 1], ALU.subtract, ALU.mult)
                    last.then_inc(xn2_ready, 1)
                if isinstance(s, int) and 0 <= s < 3:
                    weight_magnitude(s)
                if isinstance(s, int) and s == BLOCKS:
                    weight_scales()
                if isinstance(s, int) and BLOCKS <= s < BLOCKS + 3:
                    weight_parts(s - BLOCKS)

            dve.wait_ge(consts_in, 16 * (N_CONSTS - 1))
            v.tensor_scalar(bq_scaled[:], pcol_sb[:, 0:1], SCALE, None, ALU.mult).then_inc(setup_vec, 2)
            slots(dve, slot)

            def step(ins, t, n):
                ins.then_inc(route_step, 1)
                dve.wait_ge(route_step, ROUTE_STEPS * t + n)

            def over(col, n):
                return col.unsqueeze(2).broadcast_to([P, BB, n])

            def route_probs(t):
                step(v.tensor_reduce(p_sum[:], route_exp[:, t, :, :], AX.X, ALU.add), t, 1)
                step(v.reciprocal(p_inv[:], p_sum[:]), t, 2)
                step(v.tensor_tensor(prob[:], route_exp[:, t, :, :], over(p_inv[:], EXPERTS), ALU.mult), t, 3)

            def route_count(t):
                step(v.tensor_reduce(al_max[:], actor_log[:, t, :, :], AX.X, ALU.max), t, 4)
                step(v.tensor_tensor(al_less[:], actor_log[:, t, :, :], over(al_max[:], KMAX), ALU.is_lt), t, 5)
                step(v.scalar_tensor_tensor(al_cand[:], al_less[:], float(EXPERTS),
                                            iota_sb[:].unsqueeze(1).broadcast_to([P, BB, KMAX]), ALU.mult, ALU.add), t, 6)
                step(v.tensor_reduce(k_less1[:], al_cand[:], AX.X, ALU.min), t, 7)

            def route_rank(t):
                shape = [P, BB, EXPERTS, EXPERTS]
                mine = prob[:].unsqueeze(3).broadcast_to(shape)
                other = prob[:].unsqueeze(2).broadcast_to(shape)
                step(v.tensor_tensor(beats[:], other, mine, ALU.is_gt), t, 8)
                step(v.tensor_tensor(ties[:], other, mine, ALU.is_equal), t, 9)
                step(v.tensor_tensor(ties_lo[:], ties[:], tri_sb[:].unsqueeze(1).broadcast_to(shape), ALU.mult), t, 10)
                step(v.tensor_tensor(ahead[:], beats[:], ties_lo[:], ALU.add), t, 11)
                step(v.tensor_reduce(rank[:], ahead[:], AX.X, ALU.add), t, 12)

            def route_scores(t):
                step(v.tensor_tensor(chosen[:], rank[:], over(k_less1[:], EXPERTS), ALU.is_le), t, 13)
                step(v.tensor_tensor(score[:], prob[:], chosen[:], ALU.mult), t, 14)
                wait(dve, st_done, t)
                step(v.tensor_scalar(score16[:, :, 0:EXPERTS], score[:], S_SCALE, None, ALU.mult), t, 15)
                step(v.scalar_tensor_tensor(score16[:, :, EXPERTS:], score[:], S_SCALE, score16[:, :, 0:EXPERTS],
                                            ALU.mult, ALU.subtract), t, 16)

            def result(t, par):
                dve.wait_ge(yt_done, t + 1)
                if not isinstance(t, int) or t >= 2:
                    dve.wait_ge(stored[par], 8 * (t - par))
                v.tensor_tensor(out_sb[par], bank[7][:].rearrange("p (b d) -> p b d", b=BB), x2_all[:, t, :, :],
                                ALU.add).then_inc(out_ready, 1)

            def low_part(i, p):
                tile = PAIR * i + p
                dve.wait_ge(hid_hi_ready, tile + 1)
                v.tensor_tensor(hid_lo[p % HRING][:], hid[p % RING], hid_hi[p % HRING][:], ALU.subtract)\
                    .then_inc(hid_lo_ready, 1)

            def pair(i, first):
                last_pair = isinstance(i, int) and i == BLOCKS // 2 - 1
                for p in range(PAIR):
                    par, j = divmod(p, TILES)
                    t = 2 * i + par
                    tile = PAIR * i + p
                    if p >= 2 or not first:
                        low_part(i, p - 2)
                    dve.wait_ge(weighted_ready, tile + 1)
                    dve.wait_ge(up_done, tile + 1)
                    wait(dve, hid_lo_ready, tile - RING + 1)
                    v.scalar_tensor_tensor(hid[p % RING], bank[2 + p % U_BANKS][:], h_scale[:], weighted[p % RING],
                                           ALU.mult, ALU.mult).then_inc(hid_ready, 1)
                    if not (par == 1 and last_pair):
                        if j == 2:
                            route_probs(t + 1)
                        if j == 4:
                            route_count(t + 1)
                        if j == 6:
                            route_rank(t + 1)
                        if j == 8:
                            route_scores(t + 1)
                    if j == 19 and not (first and par == 0):
                        result(t - 1, 1 - par)

            dve.wait_ge(rexp_ready, 1)
            route_probs(0)
            route_count(0)
            route_rank(0)
            route_scores(0)
            pair(0, True)
            with dve.Fori(1, BLOCKS // 2 - 1) as i:
                pair(i, False)
            pair(BLOCKS // 2 - 1, False)
            for p in range(PAIR - 2, PAIR):
                low_part(BLOCKS // 2 - 1, p)
            result(BLOCKS - 1, 1)


def kernel(x, ctx_1024, L0_xattn_Wq, L0_xattn_bq, L0_xattn_Wk, L0_xattn_bk, L0_xattn_Wv, L0_xattn_bv,
           L0_ffn_router_w, L0_ffn_actor_w1, L0_ffn_actor_b1, L0_ffn_actor_w2, L0_ffn_actor_b2,
           L0_ffn_gate_w, L0_ffn_up_w, L0_ffn_down_w):
    import concourse.bacc as bacc
    from concourse.bass_utils import run_bass_kernel_spmd

    def units(w):
        w = np.asarray(w).reshape(EXPERTS, TILES, ROWS, P)
        return w.transpose(3, 1, 0, 2).reshape(P, TILES * P)

    down = np.asarray(L0_ffn_down_w).reshape(EXPERTS, P, TILES, ROWS).transpose(0, 3, 2, 1).reshape(P, TILES * P)
    pcols = np.zeros((P, 3), np.float32)
    pcols[:, 0] = L0_xattn_bq
    pcols[:, 1] = L0_xattn_bk
    pcols[:ACTOR, 2] = L0_ffn_actor_b1
    col = np.arange(P)
    arrays = {
        "x": np.asarray(x).reshape(BATCHES * P, P),
        "ctx_t": np.asarray(ctx_1024).reshape(BATCHES * CTX, P).T,
        "wcols": np.concatenate([np.asarray(w).T for w in (L0_xattn_Wq, L0_xattn_Wk, L0_xattn_Wv, L0_ffn_router_w,
                                                           L0_ffn_actor_w1)], axis=1),
        "pcols": pcols,
        "bv": np.asarray(L0_xattn_bv),
        "b2": np.asarray(L0_ffn_actor_b2),
        "w2t": np.asarray(L0_ffn_actor_w2).T,
        "gate_t": units(L0_ffn_gate_w),
        "up_t": units(L0_ffn_up_w),
        "down_t": down,
        "ident": np.eye(P, dtype=np.float32),
        "ident16": np.eye(P, dtype=np.float16),
        "sel": (np.arange(2 * EXPERTS)[:, None] % EXPERTS == col[None, :] // ROWS).astype(np.float16),
        "tri": np.broadcast_to(np.tri(EXPERTS, k=-1, dtype=np.float32), (P, EXPERTS, EXPERTS)),
        "iota": np.broadcast_to(np.arange(KMAX, dtype=np.float32), (P, KMAX)),
    }
    arrays = {n: np.ascontiguousarray(a) for n, a in arrays.items()}
    nc = bacc.Bacc("TRN2", target_bir_lowering=False, num_devices=1)
    args = [nc.dram_tensor(f"in_{n}", a.shape, mybir.dt.from_np(a.dtype), kind="ExternalInput").ap()
            for n, a in arrays.items()]
    args.append(nc.dram_tensor("out", (BATCHES * P, P), F32, kind="ExternalOutput").ap())
    program(nc, *args)
    r = run_bass_kernel_spmd(nc, [{f"in_{n}": a for n, a in arrays.items()}], core_ids=[0])
    return r.results[0]["out"].reshape(BATCHES, P, P)
```

```python
from contextlib import ExitStack

import numpy as np

import concourse.bass as bass
from concourse import mybir

F32 = mybir.dt.float32
F16 = mybir.dt.float16
U32 = mybir.dt.uint32
ALU = mybir.AluOpType
ACT = mybir.ActivationFunctionType
AX = mybir.AxisListType

P = 128
BATCHES, CTX = 64, 120
BB = 4
NT = BB * P
NC = BB * CTX
BLOCKS = BATCHES // BB
EXPERTS, HIDDEN = 8, 336
ROWS = P // EXPERTS
TILES = HIDDEN // ROWS
ACTOR, KMAX = 50, 6
EPS = 1e-5
GELU_C, GELU_A = 0.7978845608028654, 0.044715
SCALE = float(P) ** -0.5

G_BANKS, U_BANKS = 2, 3
RING, HRING = 3, 6
DOWN_LAG = 4
PAIR = 2 * TILES

W_TOP = 256.0
H_SCALE = 2.0 ** -7
S_SCALE = 256.0

ROUTE_STEPS = 16

PART = TILES // 3
WEIGHT_PARTS = ((0, 0), (1, 0), (0, 1), (1, 1), (0, 2), (1, 2), (2, 0), (2, 1), (2, 2))
GATE_UP_PARTS = 6
HI_PARTS_OF_SLOT = {BLOCKS - 2: (0, 1), BLOCKS - 1: (1, 2), BLOCKS: (2, 8), BLOCKS + 2: (8, 9)}
MAGNITUDES_OF_SLOT = {(0, 0): (0, 2), (0, 1): (2, 3), (1, 0): (3, 4), (1, 1): (4, 6), (2, 1): (6, 7),
                      (3, 0): (7, 8), (3, 1): (8, 9)}
LO_PARTS_OF_TILE = {4: 7, 9: 8}


def program(nc, x, ctx_t, consts, consts16, gate_t, up_t, down_t, out):
    x_blocks = x.rearrange("(t b p) d -> t p b d", b=BB, p=P)
    out_blocks = out.rearrange("(t b p) d -> t p b d", b=BB, p=P)
    ctx_blocks = ctx_t.rearrange("p (t n) -> t p n", n=NC)

    with ExitStack() as stack:
        def sb(name, shape, dt=F32):
            return stack.enter_context(nc.sbuf_tensor(name, shape, dt))

        def sem(name):
            return stack.enter_context(nc.semaphore(name))

        bank = [stack.enter_context(nc.psum_tensor(f"bank{k}", [P, 512], F32)) for k in range(8)]

        consts_sb = sb("consts_sb", [P, consts.shape[1]])
        start = 0

        def const(width, rows=P):
            nonlocal start
            start += width
            return consts_sb[0:rows, start - width:start]

        ident_sb = const(P)
        wq_t, wk_t, wv_t, router_t, w1_t = (const(n) for n in (P, P, P, EXPERTS, ACTOR))
        bq_col, bk_col, b1_col = const(1), const(1), const(1, ACTOR)
        w2_sb = const(KMAX, ACTOR)
        bv_sb, b2_sb, iota_sb = (const(n) for n in (P, KMAX, KMAX))
        tri_sb = const(EXPERTS * EXPERTS).rearrange("p (a b) -> p a b", a=EXPERTS)
        consts16_sb = sb("consts16_sb", [P, 2 * P], F16)
        ident16_sb = consts16_sb[:, 0:P]
        sel_sb = consts16_sb[0:2 * EXPERTS, P:]
        bq_scaled = sb("bq_scaled", [P, 1])
        eps_sb = sb("eps_sb", [P, BB])
        neg_half = sb("neg_half", [P, BB])
        work = sb("work", [P, 2 * TILES * P])
        raw = [work[:, 0:TILES * P], work[:, TILES * P:], sb("raw_down", [P, TILES * P])[:]]
        w_hi = [sb(f"{n}_hi", [P, TILES * P], F16) for n in ("gate", "up", "down")]
        w_lo = [sb(f"{n}_lo", [P, TILES * P], F16) for n in ("gate", "up", "down")]
        w_abs = sb("w_abs", [P, 3, 3])
        w_top = sb("w_top", [P, 3, 3])
        w_max = sb("w_max", [P, 3])
        w_pow = sb("w_pow", [P, 3])
        w_inv = sb("w_inv", [P, 3])
        w_mul = sb("w_mul", [P, 3])
        silu_scale = sb("silu_scale", [P, 1])
        h_scale = sb("h_scale", [P, 1])
        y_scale = sb("y_scale", [P, 2])

        x2_all = sb("x2_all", [P, BLOCKS, BB, P])
        xn_hi = sb("xn_hi", [P, BLOCKS, NT], F16)
        xn_lo = sb("xn_lo", [P, BLOCKS, NT], F16)
        route_exp = sb("route_exp", [P, BLOCKS, BB, EXPERTS])
        actor_log = sb("actor_log", [P, BLOCKS, BB, KMAX])

        x_in = [sb(f"x_in{k}", [P, BB, P]) for k in range(2)]
        ctx_in = [sb(f"ctx_in{k}", [P, NC]) for k in range(2)]
        stats1 = sb("stats1", [P, BB, 6])
        mv1 = [sb(f"mv1_{k}", [P, BB, 2]) for k in range(2)]
        ve1 = sb("ve1", [P, BB])
        rstd1 = sb("rstd1", [P, BB])
        xn_nat = [sb(f"xn_nat{k}", [P, BB, P]) for k in range(2)]
        xn_t = sb("xn_t", [P, NT])
        q_t = sb("q_t", [P, NT])
        k_t = sb("k_t", [P, NC])
        v_sb = [sb(f"v_sb{k}", [CTX, BB * P]) for k in range(2)]
        neg_max = [sb(f"neg_max{k}", [P, BB]) for k in range(2)]
        probs = sb("probs", [P, BB, CTX])
        sums = [sb(f"sums{k}", [P, BB]) for k in range(2)]
        inv_sum = sb("inv_sum", [P, BB])
        probs_t = sb("probs_t", [CTX, BB * P])
        stats2 = sb("stats2", [P, BB, 6])
        mv2 = [sb(f"mv2_{k}", [P, BB, 2]) for k in range(2)]
        ve2 = sb("ve2", [P, BB])
        rstd2 = [sb(f"rstd2_{k}", [P, BB]) for k in range(2)]
        xn2_nat = [sb(f"xn2_nat{k}", [P, BB, P]) for k in range(2)]
        xn2_t = sb("xn2_t", [P, NT])
        route_max = sb("route_max", [P, BB])
        a_sb = [sb(f"a_sb{k}", [ACTOR, NT]) for k in range(2)]
        shared = [sb(f"shared{k}", [P, NT]) for k in range(5)]
        a_sq, a_poly, a_arg, a_tanh, a_gelu2 = (buf[0:ACTOR, :] for buf in shared)
        al_raw = sb("al_raw", [P, BB, KMAX])

        silu, weighted, hid = ([work[:, (r * RING + k) * NT:(r * RING + k + 1) * NT] for k in range(RING)]
                               for r in range(3))
        hid_hi = [sb(f"hid_hi{k}", [P, NT], F16) for k in range(HRING)]
        hid_lo = [sb(f"hid_lo{k}", [P, NT], F16) for k in range(HRING)]
        p_sum = sb("p_sum", [P, BB])
        p_inv = sb("p_inv", [P, BB])
        prob = sb("prob", [P, BB, EXPERTS])
        al_max = sb("al_max", [P, BB])
        al_less = sb("al_less", [P, BB, KMAX])
        al_cand = sb("al_cand", [P, BB, KMAX])
        k_less1 = sb("k_less1", [P, BB])
        beats = sb("beats", [P, BB, EXPERTS, EXPERTS])
        ties = sb("ties", [P, BB, EXPERTS, EXPERTS])
        ties_lo = sb("ties_lo", [P, BB, EXPERTS, EXPERTS])
        ahead = sb("ahead", [P, BB, EXPERTS, EXPERTS])
        rank = sb("rank", [P, BB, EXPERTS])
        chosen = sb("chosen", [P, BB, EXPERTS])
        score = sb("score", [P, BB, EXPERTS])
        score16 = sb("score16", [P, BB, 2 * EXPERTS], F16)
        score_t = sb("score_t", [2 * EXPERTS, NT], F16)
        score_bc = [shared[k][:] for k in range(2)]
        y_sb = shared[2][:]
        out_sb = [shared[3 + k][:].rearrange("p (b d) -> p b d", b=BB) for k in range(2)]

        consts_in = sem("consts_in")
        weights_in = [sem(f"weights_in{n}") for n in range(9)]
        x_loaded = [sem(f"x_loaded{k}") for k in range(2)]
        ctx_loaded = [sem(f"ctx_loaded{k}") for k in range(2)]
        consts16_in = sem("consts16_in")
        setup_act = sem("setup_act")
        setup_pool = sem("setup_pool")
        w_stat = sem("w_stat")
        w_all = sem("w_all")
        w_chain = sem("w_chain")
        w_hi_done = sem("w_hi_done")
        w_lo_done = sem("w_lo_done")
        ln1_stats, ln1_mv, ln1_ve, ln1_rstd, xn_ready, xb_ready = (
            sem(n) for n in ("ln1_stats", "ln1_mv", "ln1_ve", "ln1_rstd", "xn_ready", "xb_ready"))
        t1_done, xnt_ready, kp_done, kt_ready, vp_done, v_ready, qp_done, qt_ready = (
            sem(n) for n in ("t1_done", "xnt_ready", "kp_done", "kt_ready", "vp_done", "v_ready", "qp_done",
                             "qt_ready"))
        e_done, max_ready, exp_done, pt_done, ptt_ready, o_done, inv_ready, x2_ready = (
            sem(n) for n in ("e_done", "max_ready", "exp_done", "pt_done", "ptt_ready", "o_done", "inv_ready",
                             "x2_ready"))
        ln2_stats, ln2_mv, ln2_ve, ln2_rstd, xn2_ready, t2_done, xn2t_ready, hi_ready, lo_ready = (
            sem(n) for n in ("ln2_stats", "ln2_mv", "ln2_ve", "ln2_rstd", "xn2_ready", "t2_done", "xn2t_ready",
                             "hi_ready", "lo_ready"))
        ah_done, a_ready, sq_ready, poly_ready, arg_ready, tanh_ready, gelu_ready, al_done, al_add, al_ready = (
            sem(n) for n in ("ah_done", "a_ready", "sq_ready", "poly_ready", "arg_ready", "tanh_ready",
                             "gelu_ready", "al_done", "al_add", "al_ready"))
        r_done, rmax_ready, rsub_ready, rexp_ready = (
            sem(n) for n in ("r_done", "rmax_ready", "rsub_ready", "rexp_ready"))
        gate_done, up_done, silu_ready, weighted_ready, hid_ready, hid_hi_ready, hid_lo_ready, down_done = (
            sem(n) for n in ("gate_done", "up_done", "silu_ready", "weighted_ready", "hid_ready", "hid_hi_ready",
                             "hid_lo_ready", "down_done"))
        route_step, st_done, st_ready, bc_done, bc_ready, y_ready, yt_done, out_ready = (
            sem(n) for n in ("route_step", "st_done", "st_ready", "bc_done", "bc_ready", "y_ready", "yt_done",
                             "out_ready"))
        stored = [sem(f"stored{k}") for k in range(2)]

        def wait(eng, s, value):
            if not isinstance(value, int) or value > 0:
                eng.wait_ge(s, value)

        def live(slot, lag):
            return not isinstance(slot, int) or 0 <= slot - lag < BLOCKS

        def weight_part(n):
            k, c = WEIGHT_PARTS[n]
            return k, slice(c * PART * P, (c + 1) * PART * P)

        def slots(eng, body):
            for s in range(-1, 4):
                body(s, s % 2)
            with eng.Fori(2, BLOCKS // 2 - 1) as i:
                body(2 * i, 0)
                body(2 * i + 1, 1)
            for s in range(BLOCKS - 2, BLOCKS + 4):
                body(s, s % 2)

        block = stack.enter_context(nc.Block())

        @block.sync
        def _(sp):
            def loads(b, par):
                wait(sp, xb_ready, b - 1)
                wait(sp, xn_ready, b - 1)
                sp.dma_start(x_in[par][:], x_blocks[b]).then_inc(x_loaded[par], 16)
                wait(sp, vp_done, b - 1)
                sp.dma_start(ctx_in[par][:], ctx_blocks[b]).then_inc(ctx_loaded[par], 16)

            loads(0, 0)
            loads(1, 1)
            for k, w in enumerate((gate_t, up_t, down_t)):
                for c in range(3):
                    cols = slice(c * PART * P, (c + 1) * PART * P)
                    sp.dma_start(raw[k][:, cols], w[:, cols]).then_inc(weights_in[3 * k + c], 16)
                if k < 2:
                    loads(2 + k, k)
            with sp.Fori(2, BLOCKS // 2) as i:
                loads(2 * i, 0)
                loads(2 * i + 1, 1)

            with sp.Fori(0, BLOCKS // 2) as i:
                for par in range(2):
                    sp.wait_ge(out_ready, 2 * i + par + 1)
                    sp.dma_start(out_blocks[2 * i + par], out_sb[par]).then_inc(stored[par], 16)
            for par in range(2):
                sp.wait_ge(stored[par], 16 * (BLOCKS // 2))

        @block.tensor
        def _(pe):
            mm = nc.tensor.matmul

            def upto(s, lag):
                return min(s - lag + 1, BLOCKS) if isinstance(s, int) else s - lag + 1

            def actor_logits(t, to_bank):
                pe.wait_ge(gelu_ready, t + 1)
                for b in range(BB):
                    last = mm(to_bank[:, b * KMAX:(b + 1) * KMAX], a_gelu2[:, b * P:(b + 1) * P], w2_sb,
                              start=True, stop=True)
                last.then_inc(al_done, 1)

            def router(s):
                pe.wait_ge(xn2t_ready, s - 2)
                wait(pe, kt_ready, upto(s, 0))
                if not live(s, 0):
                    pe.wait_ge(rsub_ready, s - 3)
                for b in range(BB):
                    last = mm(bank[1][:, NC + b * EXPERTS:NC + (b + 1) * EXPERTS], xn2_t[:, b * P:(b + 1) * P],
                              router_t, start=True, stop=True)
                last.then_inc(r_done, 1)

            def actor_hidden(s):
                pe.wait_ge(xn2t_ready, s - 2)
                wait(pe, a_ready, s - 3)
                mm(bank[7][0:ACTOR, :], w1_t, xn2_t[:], start=True, stop=True).then_inc(ah_done, 1)

            def slot(s, par):
                if live(s, 1):
                    pe.wait_ge(qt_ready, s)
                    wait(pe, exp_done, BB * (s - 1))
                    for b in range(BB):
                        last = mm(bank[4][:, b * CTX:(b + 1) * CTX], q_t[:, b * P:(b + 1) * P],
                                  k_t[:, b * CTX:(b + 1) * CTX], start=True, stop=True)
                    last.then_inc(e_done, 1)
                if live(s, 2):
                    pe.wait_ge(ptt_ready, s - 1)
                    pe.wait_ge(v_ready, s - 1)
                    wait(pe, x2_ready, s - 2)
                    for b in range(BB):
                        last = mm(bank[6][:, b * P:(b + 1) * P], probs_t[:, b * P:(b + 1) * P],
                                  v_sb[par][:, b * P:(b + 1) * P], start=True, stop=True)
                    last.then_inc(o_done, 1)
                if live(s, 0):
                    pe.wait_ge(xn_ready, s + 1)
                    wait(pe, xn2t_ready, s - 3)
                    for b in range(BB):
                        last = nc.tensor.transpose(bank[0][:, b * P:(b + 1) * P], xn_nat[par][:, b, :], ident_sb)
                    last.then_inc(t1_done, 1)
                    pe.wait_ge(ctx_loaded[par], 8 * (s - par) + 16)
                    wait(pe, kt_ready, s)
                    wait(pe, rsub_ready, s - 3)
                    mm(bank[1][:, 0:NC], wk_t, ctx_in[par][:], start=True, stop=True).then_inc(kp_done, 1)
                    wait(pe, v_ready, s)
                    for b in range(BB):
                        last = mm(bank[2][0:CTX, b * P:(b + 1) * P], ctx_in[par][:, b * CTX:(b + 1) * CTX], wv_t,
                                  start=True, stop=True)
                    last.then_inc(vp_done, 1)
                if live(s, 3):
                    pe.wait_ge(xn2_ready, s - 2)
                    wait(pe, xnt_ready, upto(s, 0))
                    for b in range(BB):
                        last = nc.tensor.transpose(bank[0][:, b * P:(b + 1) * P], xn2_nat[1 - par][:, b, :], ident_sb)
                    last.then_inc(t2_done, 1)
                if live(s, 0):
                    pe.wait_ge(xnt_ready, s + 1)
                    wait(pe, qt_ready, s)
                    wait(pe, al_add, s - 4)
                    mm(bank[3][:], wq_t, xn_t[:], start=True, stop=True).then_inc(qp_done, 1)
                if live(s, 1):
                    pe.wait_ge(exp_done, BB * s)
                    wait(pe, ptt_ready, s - 1)
                    for b in range(BB):
                        last = nc.tensor.transpose(bank[5][0:CTX, b * P:(b + 1) * P], probs[:, b, :], ident_sb)
                    last.then_inc(pt_done, 1)
                if live(s, 3):
                    if live(s, 0):
                        router(s)
                        actor_hidden(s)
                    else:
                        actor_hidden(s)
                        router(s)
                if live(s, 4) and live(s, 2):
                    wait(pe, qt_ready, upto(s, 0))
                    actor_logits(s - 4, bank[3])

            pe.wait_ge(consts_in, 16)
            slots(pe, slot)

            def score_transposes(t):
                pe.wait_ge(route_step, ROUTE_STEPS * (t + 1))
                wait(pe, out_ready, t - 2)
                for b in range(BB):
                    last = nc.tensor.transpose(bank[7][0:2 * EXPERTS, :].bitcast(F16)[:, b * P:(b + 1) * P],
                                               score16[:, b, :], ident16_sb)
                last.then_inc(st_done, 1)

            def score_broadcast(t):
                pe.wait_ge(st_ready, t + 1)
                mm(bank[7][:], sel_sb, score_t[:], start=True, stop=True).then_inc(bc_done, 1)

            def result_transposes(t):
                pe.wait_ge(y_ready, t + 1)
                wait(pe, bc_ready, t + 3 if not isinstance(t, int) else min(t + 3, BLOCKS))
                for b in range(BB):
                    last = nc.tensor.transpose(bank[7][:, b * P:(b + 1) * P], y_sb[:, b * P:(b + 1) * P], ident_sb)
                last.then_inc(yt_done, 1)

            def split_product(dst, w, tile, hi, lo, start, stop):
                cols = slice(tile * P, (tile + 1) * P)
                mm(dst, w_hi[w][:, cols], lo, start=start, stop=False)
                mm(dst, w_lo[w][:, cols], hi, start=False, stop=False)
                return mm(dst, w_hi[w][:, cols], hi, start=False, stop=stop)

            def down(i, p):
                j, par = p % TILES, (p // TILES) % 2
                tile = PAIR * i + p
                pe.wait_ge(hid_lo_ready, tile + 1)
                if j == 0:
                    wait(pe, y_ready, 2 * i + par - 1)
                split_product(bank[5 + par][:], 2, j, hid_hi[p % HRING][:], hid_lo[p % HRING][:],
                              j == 0, j == TILES - 1).then_inc(down_done, 1)

            def pair(i, first):
                for p in range(PAIR):
                    par, j = divmod(p, TILES)
                    t = 2 * i + par
                    tile = PAIR * i + p
                    part, of_part = divmod(p, PART)
                    new_part = first and par == 0 and of_part == 0
                    if new_part:
                        pe.wait_ge(w_lo_done, 2 * part + 1)
                    wait(pe, silu_ready, tile - G_BANKS + 1)
                    split_product(bank[p % G_BANKS][:], 0, j, xn_hi[:, t, :], xn_lo[:, t, :], True, True)\
                        .then_inc(gate_done, 1)
                    if new_part:
                        pe.wait_ge(w_lo_done, 2 * part + 2)
                    if first and p == 2:
                        pe.wait_ge(al_add, BLOCKS - 1)
                    wait(pe, hid_ready, tile - U_BANKS + 1)
                    split_product(bank[2 + p % U_BANKS][:], 1, j, xn_hi[:, t, :], xn_lo[:, t, :], True, True)\
                        .then_inc(up_done, 1)
                    if p >= DOWN_LAG or not first:
                        if first and p - DOWN_LAG < TILES and (p - DOWN_LAG) % PART == 0:
                            pe.wait_ge(w_lo_done, GATE_UP_PARTS + (p - DOWN_LAG) // PART + 1)
                        down(i, p - DOWN_LAG)
                    if first and p == 0:
                        score_broadcast(0)
                        actor_logits(BLOCKS - 2, bank[4])
                    if first and p == 3:
                        pe.wait_ge(bc_ready, 1)
                        actor_logits(BLOCKS - 1, bank[7])
                    if j == 12 and not (par == 1 and isinstance(i, int) and i == BLOCKS // 2 - 1):
                        score_transposes(t + 1)
                    if j == 14 and not (par == 1 and isinstance(i, int) and i == BLOCKS // 2 - 1):
                        score_broadcast(t + 1)
                    if j == 18 and not (first and par == 0):
                        result_transposes(t - 1)

            pe.wait_ge(lo_ready, BLOCKS)
            pe.wait_ge(hi_ready, BLOCKS)
            pe.wait_ge(al_ready, BLOCKS - 2)
            pe.wait_ge(rsub_ready, BLOCKS)
            pe.wait_ge(x2_ready, BLOCKS)
            pe.wait_ge(a_ready, BLOCKS)
            pe.wait_ge(consts16_in, 16)
            score_transposes(0)
            pair(0, True)
            with pe.Fori(1, BLOCKS // 2 - 1) as i:
                pair(i, False)
            pair(BLOCKS // 2 - 1, False)
            for p in range(PAIR - DOWN_LAG, PAIR):
                down(BLOCKS // 2 - 1, p)
            result_transposes(BLOCKS - 1)

        @block.scalar
        def _(act):
            af = nc.scalar.activation

            def weight_high(n):
                k, cols = weight_part(n)
                act.wait_ge(w_chain, 5)
                af(w_hi[k][:, cols], raw[k][:, cols], ACT.Copy, scale=w_mul[:, k:k + 1]).then_inc(w_hi_done, 1)

            def tanh(t):
                act.wait_ge(arg_ready, t + 1)
                wait(act, gelu_ready, t)
                af(a_tanh, a_arg, ACT.Tanh, scale=GELU_C).then_inc(tanh_ready, 1)

            def slot(s, par):
                if live(s, 0):
                    act.wait_ge(t1_done, s + 1)
                    wait(act, qp_done, s)
                    af(xn_t[:], bank[0][:], ACT.Copy).then_inc(xnt_ready, 1)
                if live(s, 1):
                    pe_prev = 1 - par
                    act.wait_ge(max_ready, s)
                    wait(act, pt_done, s - 1)
                    wait(act, inv_ready, s - 2)
                    for b in range(BB):
                        af(probs[:, b, :], bank[4][:, b * CTX:(b + 1) * CTX], ACT.Exp, bias=neg_max[pe_prev][:, b:b + 1],
                           accum_out=sums[pe_prev][:, b:b + 1]).then_inc(exp_done, 1)
                if live(s, 0):
                    act.wait_ge(kp_done, s + 1)
                    wait(act, e_done, s)
                    af(k_t[:], bank[1][:, 0:NC], ACT.Identity, bias=bk_col).then_inc(kt_ready, 1)
                if live(s, 3):
                    act.wait_ge(t2_done, s - 2)
                    wait(act, ah_done, s - 3)
                    wait(act, hi_ready, s - 3)
                    wait(act, lo_ready, s - 3)
                    af(xn2_t[:], bank[0][:], ACT.Copy).then_inc(xn2t_ready, 1)
                if live(s, 4) and live(s, 3):
                    tanh(s - 4)
                if live(s, 0):
                    act.wait_ge(qp_done, s + 1)
                    af(q_t[:], bank[3][:], ACT.Identity, bias=bq_scaled[:], scale=SCALE).then_inc(qt_ready, 1)
                if live(s, 4):
                    act.wait_ge(rsub_ready, s - 3)
                    af(route_exp[:, s - 4, :, :], route_exp[:, s - 4, :, :], ACT.Exp).then_inc(rexp_ready, 1)
                if live(s, 1):
                    act.wait_ge(pt_done, s)
                    wait(act, o_done, s - 1)
                    af(probs_t[:], bank[5][0:CTX, :], ACT.Copy).then_inc(ptt_ready, 1)
                if live(s, 3):
                    act.wait_ge(ah_done, s - 2)
                    wait(act, gelu_ready, s - 4)
                    af(a_sb[1 - par][:], bank[7][0:ACTOR, :], ACT.Identity, bias=b1_col)\
                        .then_inc(a_ready, 1)
                    act.wait_ge(a_ready, s - 2)
                    wait(act, poly_ready, s - 3)
                    af(a_sq, a_sb[1 - par][:], ACT.Square, scale=GELU_A ** 0.5).then_inc(sq_ready, 1)
                if isinstance(s, int):
                    for n in range(*HI_PARTS_OF_SLOT.get(s, (0, 0))):
                        weight_high(n)

            def score_copy(t):
                act.wait_ge(st_done, t + 1)
                wait(act, bc_done, t)
                af(score_t[:], bank[7][0:2 * EXPERTS, :].bitcast(F16)[:, 0:NT], ACT.Copy).then_inc(st_ready, 1)

            def score_spread(t, par):
                act.wait_ge(bc_done, t + 1)
                wait(act, weighted_ready, TILES * (t - 1))
                af(score_bc[par], bank[7][:], ACT.Copy, scale=1.0 / S_SCALE).then_inc(bc_ready, 1)

            def result_copy(t, par):
                act.wait_ge(down_done, TILES * (t + 1))
                wait(act, yt_done, t)
                af(y_sb, bank[5 + par][:], ACT.Copy, scale=y_scale[:, 1:2]).then_inc(y_ready, 1)

            def high_part(i, p):
                tile = PAIR * i + p
                act.wait_ge(hid_ready, tile + 1)
                wait(act, down_done, tile - HRING + 1)
                af(hid_hi[p % HRING][:], hid[p % RING], ACT.Copy).then_inc(hid_hi_ready, 1)

            def pair(i, first):
                for p in range(PAIR):
                    par, j = divmod(p, TILES)
                    t = 2 * i + par
                    tile = PAIR * i + p
                    act.wait_ge(gate_done, tile + 1)
                    wait(act, weighted_ready, tile - RING + 1)
                    af(silu[p % RING], bank[p % G_BANKS][:], ACT.Silu, scale=silu_scale[:]).then_inc(silu_ready, 1)
                    if p >= 2 or not first:
                        high_part(i, p - 2)
                    if j == 12 and not (par == 1 and isinstance(i, int) and i == BLOCKS // 2 - 1):
                        score_copy(t + 1)
                    if j == 14 and not (par == 1 and isinstance(i, int) and i == BLOCKS // 2 - 1):
                        score_spread(t + 1, 1 - par)
                    if j == DOWN_LAG + 1 and not (first and par == 0):
                        result_copy(t - 1, 1 - par)

            act.dma_start(consts_sb[:], consts).then_inc(consts_in, 16)
            act.dma_start(consts16_sb[:], consts16).then_inc(consts16_in, 16)
            act.wait_ge(consts_in, 16)
            af(bq_scaled[:], bq_col, ACT.Copy, scale=SCALE).then_inc(setup_act, 1)
            act.wait_ge(setup_act, 1)
            nc.scalar.preload_act_table(ACT.Exp)
            slots(act, slot)
            nc.scalar.preload_act_table(ACT.Silu)
            tanh(BLOCKS - 1)
            act.wait_ge(w_chain, 7)
            score_copy(0)
            score_spread(0, 0)
            act.wait_ge(w_lo_done, GATE_UP_PARTS)
            pair(0, True)
            with act.Fori(1, BLOCKS // 2 - 1) as i:
                pair(i, False)
            pair(BLOCKS // 2 - 1, False)
            for p in range(PAIR - 2, PAIR):
                high_part(BLOCKS // 2 - 1, p)
            result_copy(BLOCKS - 1, 1)

        @block.gpsimd
        def _(pool):
            g = nc.gpsimd
            g.memset(eps_sb[:], EPS).then_inc(setup_pool, 1)
            g.memset(neg_half[:], -0.5).then_inc(setup_pool, 1)
            pool.wait_ge(setup_pool, 2)
            pool.wait_ge(consts_in, 16)

            def slot(s, par):
                nxt = 1 - par
                if live(s, 4):
                    pool.wait_ge(sq_ready, s - 3)
                    wait(pool, arg_ready, s - 4)
                    g.tensor_tensor(a_poly, a_sq, a_sb[par][:], ALU.mult).then_inc(poly_ready, 1)
                    pool.wait_ge(poly_ready, s - 3)
                    wait(pool, tanh_ready, s - 4)
                    g.tensor_tensor(a_arg, a_poly, a_sb[par][:], ALU.add).then_inc(arg_ready, 1)
                if live(s, 0):
                    g.tensor_tensor(x2_all[:, s, :, :], x_in[par][:],
                                    bv_sb.unsqueeze(1).broadcast_to([P, BB, P]), ALU.add).then_inc(xb_ready, 1)
                if live(s, -1):
                    pool.wait_ge(ln1_mv, s + 2)
                    wait(pool, ln1_rstd, s + 1)
                    g.tensor_tensor(ve1[:], mv1[nxt][:, :, 1], eps_sb[:], ALU.add).then_inc(ln1_ve, 1)
                    pool.wait_ge(ln1_ve, s + 2)
                    wait(pool, xn_ready, s + 1)
                    g.tensor_tensor(rstd1[:], ve1[:], neg_half[:], ALU.pow).then_inc(ln1_rstd, 1)
                if live(s, 2):
                    pool.wait_ge(ln2_mv, s - 1)
                    wait(pool, ln2_rstd, s - 2)
                    g.tensor_tensor(ve2[:], mv2[par][:, :, 1], eps_sb[:], ALU.add).then_inc(ln2_ve, 1)
                    pool.wait_ge(ln2_ve, s - 1)
                    wait(pool, xn2_ready, s - 3)
                    g.tensor_tensor(rstd2[par][:], ve2[:], neg_half[:], ALU.pow).then_inc(ln2_rstd, 1)
                if live(s, 3):
                    pool.wait_ge(hi_ready, s - 2)
                    g.tensor_tensor(xn_lo[:, s - 3, :], xn2_t[:], xn_hi[:, s - 3, :], ALU.subtract).then_inc(lo_ready, 1)
                if isinstance(s, int) and s == 3:
                    pool.wait_ge(w_stat, 9)
                    g.partition_all_reduce(w_top[:].rearrange("p k c -> p (k c)"), w_abs[:].rearrange("p k c -> p (k c)"), P,
                                            bass.bass_isa.ReduceOp.max).then_inc(w_all, 1)

            slots(pool, slot)

            with pool.Fori(0, BLOCKS // 2) as i:
                for p in range(PAIR):
                    par, j = divmod(p, TILES)
                    tile = PAIR * i + p
                    if j == 0:
                        pool.wait_ge(bc_ready, 2 * i + par + 1)
                    pool.wait_ge(silu_ready, tile + 1)
                    pool.wait_ge(up_done, tile + 1)
                    g.tensor_tensor(weighted[p % RING], silu[p % RING], score_bc[par], ALU.mult)\
                        .then_inc(weighted_ready, 1)

        @block.vector
        def _(dve):
            v = nc.vector

            def weight_magnitude(n):
                k, c = divmod(n, 3)
                dve.wait_ge(weights_in[n], 16)
                v.tensor_reduce(w_abs[:, k, c:c + 1], raw[k][:, c * PART * P:(c + 1) * PART * P], AX.X, ALU.max,
                                apply_absolute_value=True).then_inc(w_stat, 1)

            def weight_magnitudes(s, place):
                if isinstance(s, int):
                    for n in range(*MAGNITUDES_OF_SLOT.get((s, place), (0, 0))):
                        weight_magnitude(n)

            def weight_scales():
                dve.wait_ge(w_all, 1)
                v.tensor_reduce(w_max[:], w_top[:], AX.X, ALU.max).then_inc(w_chain, 1)
                dve.wait_ge(w_chain, 1)
                v.tensor_scalar(w_pow[:], w_max[:], 1e-30, None, ALU.max).then_inc(w_chain, 1)
                dve.wait_ge(w_chain, 2)
                v.tensor_scalar(w_pow[:].bitcast(U32), w_pow[:].bitcast(U32), 0x7F800000, None, ALU.bitwise_and)\
                    .then_inc(w_chain, 1)
                dve.wait_ge(w_chain, 3)
                v.reciprocal(w_inv[:], w_pow[:]).then_inc(w_chain, 1)
                dve.wait_ge(w_chain, 4)
                v.tensor_scalar(w_mul[:], w_inv[:], W_TOP / 2, None, ALU.mult).then_inc(w_chain, 1)
                v.tensor_scalar(silu_scale[:], w_pow[:, 0:1], 2 / W_TOP, None, ALU.mult)
                v.tensor_scalar(h_scale[:], w_inv[:, 0:1], H_SCALE / 2, None, ALU.mult)
                v.tensor_tensor(y_scale[:, 0:1], w_pow[:, 0:1], w_pow[:, 1:2], ALU.mult).then_inc(w_chain, 1)
                dve.wait_ge(w_chain, 6)
                v.tensor_scalar(y_scale[:, 1:2], y_scale[:, 0:1], w_pow[:, 2:3], 8.0 / (W_TOP * W_TOP * H_SCALE),
                                ALU.mult, ALU.mult).then_inc(w_chain, 1)

            def weight_low(n):
                k, cols = weight_part(n)
                dve.wait_ge(w_hi_done, n + 1)
                v.scalar_tensor_tensor(w_lo[k][:, cols], raw[k][:, cols], w_mul[:, k:k + 1], w_hi[k][:, cols],
                                       ALU.mult, ALU.subtract).then_inc(w_lo_done, 1)

            def row_max(t, p):
                dve.wait_ge(e_done, t + 1)
                wait(dve, exp_done, BB * (t - 1))
                v.tensor_reduce(neg_max[p][:], bank[4][:, 0:NC].rearrange("p (b n) -> p b n", b=BB), AX.X,
                                ALU.max, negate=True).then_inc(max_ready, 1)

            def norm2(t, p):
                dve.wait_ge(ln2_rstd, t + 1)
                wait(dve, t2_done, t - 1)
                for b in range(BB):
                    last = v.tensor_scalar(xn2_nat[p][:, b, :], x2_all[:, t, b, :], mv2[p][:, b, 0:1],
                                           rstd2[p][:, b:b + 1], ALU.subtract, ALU.mult)
                last.then_inc(xn2_ready, 1)

            def residual(t, p):
                wait(dve, x2_ready, t)
                v.reciprocal(inv_sum[:], sums[p][:]).then_inc(inv_ready, 1)
                dve.wait_ge(o_done, t + 1)
                dve.wait_ge(xb_ready, t + 1)
                dve.wait_ge(inv_ready, t + 1)
                for b in range(BB):
                    last = v.scalar_tensor_tensor(x2_all[:, t, b, :], bank[6][:, b * P:(b + 1) * P],
                                                  inv_sum[:, b:b + 1], x2_all[:, t, b, :], ALU.mult, ALU.add)
                last.then_inc(x2_ready, 1)

            def stats_1(t, p):
                wait(dve, ln1_mv, t)
                dve.wait_ge(x_loaded[p], 8 * (t - p) + 16)
                for b in range(BB):
                    last = v.bn_stats(stats1[:, b, :], x_in[p][:, b, :])
                last.then_inc(ln1_stats, 1)
                dve.wait_ge(ln1_stats, t + 1)
                wait(dve, xn_ready, t - 1)

            def aggregate_1(t, p):
                for b in range(BB):
                    last = v.bn_aggr(mv1[p][:, b, :], stats1[:, b, :])
                last.then_inc(ln1_mv, 1)

            def norm1(t, p):
                dve.wait_ge(ln1_rstd, t + 1)
                wait(dve, t1_done, t - 1)
                for b in range(BB):
                    last = v.tensor_scalar(xn_nat[p][:, b, :], x_in[p][:, b, :], mv1[p][:, b, 0:1],
                                           rstd1[:, b:b + 1], ALU.subtract, ALU.mult)
                last.then_inc(xn_ready, 1)

            def stats_2_waits(t):
                dve.wait_ge(x2_ready, t + 1)
                wait(dve, ln2_mv, t)

            def stats_2(t):
                for b in range(BB):
                    last = v.bn_stats(stats2[:, b, :], x2_all[:, t, b, :])
                last.then_inc(ln2_stats, 1)
                dve.wait_ge(ln2_stats, t + 1)
                wait(dve, xn2_ready, t - 1)

            def aggregate_2(t, p):
                for b in range(BB):
                    last = v.bn_aggr(mv2[p][:, b, :], stats2[:, b, :])
                last.then_inc(ln2_mv, 1)

            def values(t, p):
                dve.wait_ge(vp_done, t + 1)
                wait(dve, o_done, t - 1)
                v.tensor_copy(v_sb[p][:], bank[2][0:CTX, :]).then_inc(v_ready, 1)

            def gelu(t, p):
                dve.wait_ge(tanh_ready, t + 1)
                wait(dve, al_done, t)
                v.scalar_tensor_tensor(a_gelu2, a_tanh, 1.0, a_sb[p][:], ALU.add, ALU.mult).then_inc(gelu_ready, 1)

            def actor_logits(t, of_bank):
                dve.wait_ge(al_done, t + 1)
                wait(dve, al_ready, t)
                v.scalar_tensor_tensor(al_raw[:], of_bank[:, 0:BB * KMAX].rearrange("p (b k) -> p b k", b=BB), 0.5,
                                       b2_sb.unsqueeze(1).broadcast_to([P, BB, KMAX]), ALU.mult, ALU.add)\
                    .then_inc(al_add, 1)
                dve.wait_ge(al_add, t + 1)
                v.tensor_scalar(actor_log[:, t, :, :], al_raw[:], -30.0, 30.0, ALU.max, ALU.min).then_inc(al_ready, 1)

            router_logits = bank[1][:, NC:NC + BB * EXPERTS].rearrange("p (b e) -> p b e", b=BB)

            def router_max(t):
                dve.wait_ge(r_done, t + 1)
                wait(dve, rsub_ready, t)
                v.tensor_reduce(route_max[:], router_logits, AX.X, ALU.max).then_inc(rmax_ready, 1)

            def router_less_max(t):
                dve.wait_ge(rmax_ready, t + 1)
                v.tensor_tensor(route_exp[:, t, :, :], router_logits,
                                route_max[:].unsqueeze(2).broadcast_to([P, BB, EXPERTS]), ALU.subtract)\
                    .then_inc(rsub_ready, 1)

            def high(t):
                dve.wait_ge(xn2t_ready, t + 1)
                v.tensor_copy(xn_hi[:, t, :], xn2_t[:]).then_inc(hi_ready, 1)

            def slot(s, par):
                nxt = 1 - par
                if isinstance(s, int) and s >= BLOCKS:
                    return
                if live(s, 1):
                    row_max(s - 1, nxt)
                if live(s, 3):
                    norm2(s - 3, nxt)
                if live(s, 2):
                    residual(s - 2, par)
                if live(s, -1):
                    stats_1(s + 1, nxt)
                if live(s, 2):
                    stats_2_waits(s - 2)
                weight_magnitudes(s, 0)
                if live(s, 0):
                    values(s, par)
                if live(s, -1):
                    aggregate_1(s + 1, nxt)
                if live(s, 4):
                    gelu(s - 4, par)
                if live(s, 2):
                    stats_2(s - 2)
                if live(s, 3):
                    router_max(s - 3)
                if live(s, 2):
                    aggregate_2(s - 2, par)
                if live(s, 3):
                    router_less_max(s - 3)
                weight_magnitudes(s, 1)
                if live(s, -1):
                    norm1(s + 1, nxt)
                if live(s, 3):
                    high(s - 3)
                if live(s, 4):
                    actor_logits(s - 4, bank[3])
                if isinstance(s, int) and s == BLOCKS - 2:
                    weight_scales()

            def drain():
                z = BLOCKS - 1
                row_max(z, 1)
                norm2(z - 2, 1)
                residual(z - 1, 0)
                dve.wait_ge(rexp_ready, 1)
                route_probs(0)
                route_count(0)
                gelu(z - 3, 0)
                stats_2_waits(z - 1)
                stats_2(z - 1)
                router_max(z - 2)
                aggregate_2(z - 1, 0)
                router_less_max(z - 2)
                high(z - 2)
                actor_logits(z - 3, bank[3])
                route_rank(0)
                residual(z, 1)
                stats_2_waits(z)
                stats_2(z)
                aggregate_2(z, 1)
                norm2(z - 1, 0)
                gelu(z - 2, 1)
                high(z - 1)
                norm2(z, 1)
                router_max(z - 1)
                router_less_max(z - 1)
                weight_low(0)
                weight_low(1)
                high(z)
                gelu(z - 1, 0)
                route_scores(0)
                actor_logits(z - 2, bank[3])
                router_max(z)
                router_less_max(z)
                weight_low(2)
                weight_low(3)
                weight_low(4)
                weight_low(5)
                actor_logits(z - 1, bank[4])
                gelu(z, 1)
                weight_low(6)

            def step(ins, t, n):
                ins.then_inc(route_step, 1)
                dve.wait_ge(route_step, ROUTE_STEPS * t + n)

            def over(col, n):
                return col.unsqueeze(2).broadcast_to([P, BB, n])

            def route_probs(t):
                step(v.tensor_reduce(p_sum[:], route_exp[:, t, :, :], AX.X, ALU.add), t, 1)
                step(v.reciprocal(p_inv[:], p_sum[:]), t, 2)
                step(v.tensor_tensor(prob[:], route_exp[:, t, :, :], over(p_inv[:], EXPERTS), ALU.mult), t, 3)

            def route_count(t):
                step(v.tensor_reduce(al_max[:], actor_log[:, t, :, :], AX.X, ALU.max), t, 4)
                step(v.tensor_tensor(al_less[:], actor_log[:, t, :, :], over(al_max[:], KMAX), ALU.is_lt), t, 5)
                step(v.scalar_tensor_tensor(al_cand[:], al_less[:], float(EXPERTS),
                                            iota_sb.unsqueeze(1).broadcast_to([P, BB, KMAX]), ALU.mult, ALU.add), t, 6)
                step(v.tensor_reduce(k_less1[:], al_cand[:], AX.X, ALU.min), t, 7)

            def route_rank(t):
                shape = [P, BB, EXPERTS, EXPERTS]
                mine = prob[:].unsqueeze(3).broadcast_to(shape)
                other = prob[:].unsqueeze(2).broadcast_to(shape)
                step(v.tensor_tensor(beats[:], other, mine, ALU.is_gt), t, 8)
                step(v.tensor_tensor(ties[:], other, mine, ALU.is_equal), t, 9)
                step(v.tensor_tensor(ties_lo[:], ties[:], tri_sb.unsqueeze(1).broadcast_to(shape), ALU.mult), t, 10)
                step(v.tensor_tensor(ahead[:], beats[:], ties_lo[:], ALU.add), t, 11)
                step(v.tensor_reduce(rank[:], ahead[:], AX.X, ALU.add), t, 12)

            def route_scores(t):
                step(v.tensor_tensor(chosen[:], rank[:], over(k_less1[:], EXPERTS), ALU.is_le), t, 13)
                step(v.tensor_tensor(score[:], prob[:], chosen[:], ALU.mult), t, 14)
                wait(dve, st_done, t)
                step(v.tensor_scalar(score16[:, :, 0:EXPERTS], score[:], S_SCALE, None, ALU.mult), t, 15)
                step(v.scalar_tensor_tensor(score16[:, :, EXPERTS:], score[:], S_SCALE, score16[:, :, 0:EXPERTS],
                                            ALU.mult, ALU.subtract), t, 16)

            def result(t, par):
                dve.wait_ge(yt_done, t + 1)
                if not isinstance(t, int) or t >= 2:
                    dve.wait_ge(stored[par], 8 * (t - par))
                v.tensor_tensor(out_sb[par], bank[7][:].rearrange("p (b d) -> p b d", b=BB), x2_all[:, t, :, :],
                                ALU.add).then_inc(out_ready, 1)

            def low_part(i, p):
                tile = PAIR * i + p
                dve.wait_ge(hid_hi_ready, tile + 1)
                v.tensor_tensor(hid_lo[p % HRING][:], hid[p % RING], hid_hi[p % HRING][:], ALU.subtract)\
                    .then_inc(hid_lo_ready, 1)

            def pair(i, first):
                last_pair = isinstance(i, int) and i == BLOCKS // 2 - 1
                for p in range(PAIR):
                    par, j = divmod(p, TILES)
                    t = 2 * i + par
                    tile = PAIR * i + p
                    if p >= 2 or not first:
                        low_part(i, p - 2)
                    dve.wait_ge(weighted_ready, tile + 1)
                    dve.wait_ge(up_done, tile + 1)
                    wait(dve, hid_lo_ready, tile - RING + 1)
                    v.scalar_tensor_tensor(hid[p % RING], bank[2 + p % U_BANKS][:], h_scale[:], weighted[p % RING],
                                           ALU.mult, ALU.mult).then_inc(hid_ready, 1)
                    if first and p == 4:
                        actor_logits(BLOCKS - 1, bank[7])
                    if first and p in LO_PARTS_OF_TILE:
                        weight_low(LO_PARTS_OF_TILE[p])
                    if not (par == 1 and last_pair):
                        if j == 2:
                            route_probs(t + 1)
                        if j == 4:
                            route_count(t + 1)
                        if j == 6:
                            route_rank(t + 1)
                        if j == 8:
                            route_scores(t + 1)
                    if j == 19 and not (first and par == 0):
                        result(t - 1, 1 - par)

            slots(dve, slot)
            drain()
            pair(0, True)
            with dve.Fori(1, BLOCKS // 2 - 1) as i:
                pair(i, False)
            pair(BLOCKS // 2 - 1, False)
            for p in range(PAIR - 2, PAIR):
                low_part(BLOCKS // 2 - 1, p)
            result(BLOCKS - 1, 1)


def kernel(x, ctx_1024, L0_xattn_Wq, L0_xattn_bq, L0_xattn_Wk, L0_xattn_bk, L0_xattn_Wv, L0_xattn_bv,
           L0_ffn_router_w, L0_ffn_actor_w1, L0_ffn_actor_b1, L0_ffn_actor_w2, L0_ffn_actor_b2,
           L0_ffn_gate_w, L0_ffn_up_w, L0_ffn_down_w):
    import concourse.bacc as bacc
    from concourse.bass_utils import run_bass_kernel_spmd

    def units(w):
        w = np.asarray(w).reshape(EXPERTS, TILES, ROWS, P)
        return w.transpose(3, 1, 0, 2).reshape(P, TILES * P)

    down = np.asarray(L0_ffn_down_w).reshape(EXPERTS, P, TILES, ROWS).transpose(0, 3, 2, 1).reshape(P, TILES * P)
    col = np.arange(P)

    def rows(a, n=P):
        a = np.asarray(a)
        if a.ndim == 1:
            return np.broadcast_to(a, (n, a.size))
        return np.concatenate([a, np.zeros((n - a.shape[0], a.shape[1]), a.dtype)])

    consts = [np.eye(P, dtype=np.float32)]
    consts += [np.asarray(w).T for w in (L0_xattn_Wq, L0_xattn_Wk, L0_xattn_Wv, L0_ffn_router_w, L0_ffn_actor_w1)]
    consts += [rows(np.asarray(b)[:, None]) for b in (L0_xattn_bq, L0_xattn_bk, L0_ffn_actor_b1)]
    consts += [rows(np.asarray(L0_ffn_actor_w2).T), rows(L0_xattn_bv), rows(L0_ffn_actor_b2)]
    consts += [rows(np.arange(KMAX, dtype=np.float32)), rows(np.tri(EXPERTS, k=-1, dtype=np.float32).reshape(-1))]
    consts16 = [np.eye(P, dtype=np.float16),
                rows((np.arange(2 * EXPERTS)[:, None] % EXPERTS == col[None, :] // ROWS).astype(np.float16))]
    arrays = {
        "x": np.asarray(x).reshape(BATCHES * P, P),
        "ctx_t": np.asarray(ctx_1024).reshape(BATCHES * CTX, P).T,
        "consts": np.concatenate(consts, axis=1),
        "consts16": np.concatenate(consts16, axis=1),
        "gate_t": units(L0_ffn_gate_w),
        "up_t": units(L0_ffn_up_w),
        "down_t": down,
    }
    arrays = {n: np.ascontiguousarray(a) for n, a in arrays.items()}
    nc = bacc.Bacc("TRN2", target_bir_lowering=False, num_devices=1)
    args = [nc.dram_tensor(f"in_{n}", a.shape, mybir.dt.from_np(a.dtype), kind="ExternalInput").ap()
            for n, a in arrays.items()]
    args.append(nc.dram_tensor("out", (BATCHES * P, P), F32, kind="ExternalOutput").ap())
    program(nc, *args)
    r = run_bass_kernel_spmd(nc, [{f"in_{n}": a for n, a in arrays.items()}], core_ids=[0])
    return r.results[0]["out"].reshape(BATCHES, P, P)
```
